# Optimizing a Trainium2 kernel written in Bass

```python
import numpy as np
import jax
import jax.numpy as jnp

def _softmax(x, axis=-1):
    return jax.nn.softmax(x, axis=axis)

def _gelu(x):
    return jax.nn.gelu(x, approximate=True)

def _silu(x):
    return jax.nn.silu(x)

def _sigmoid(x):
    return jax.nn.sigmoid(x)

def _layernorm(x, axis=-1, eps=1e-05):
    m = jnp.mean(x, axis=axis, keepdims=True)
    v = jnp.var(x, axis=axis, keepdims=True)
    return (x - m) / jnp.sqrt(v + eps)

def _scatter_add(tgt, idx, src, axis=0):
    return tgt.at[idx].add(src)

def _segment_sum(src, seg, n):
    return jax.ops.segment_sum(src, seg, n)
kernel_name = 'mk_dlrm_tower_d1_rec_r8_42a78f'

def setup_inputs(seed: int=0):
    np.random.seed(seed)
    _w = jnp.asarray

    def _rec_inputs():
        import jax
        import jax.numpy as jnp
        _tk = jax.random.key(seed)
        dense_ctx = jax.random.normal(jax.random.fold_in(_tk, 190), (2048, 16), jnp.float32)
        ids = jnp.stack([jax.random.randint(jax.random.fold_in(_tk, 200 + f), (2048,), 0, v, jnp.int32) for f, v in enumerate([125000, 12500, 1000, 12500, 12500, 1000, 12500, 12500, 1250, 12500, 1000, 1000, 1250, 1250, 12500, 12500, 1250, 12500, 12500, 125000, 1250, 1250, 12500, 1000, 12500, 12500, 1000, 1000, 1250, 1250, 1000, 1000, 1000, 12500, 1000, 1250, 1000, 1250, 1000, 1000])], axis=1)
        tbl_0 = 0.05 * jax.random.normal(jax.random.fold_in(_tk, 500 + 0), (125000, 64), jnp.float32)
        tbl_1 = 0.05 * jax.random.normal(jax.random.fold_in(_tk, 500 + 1), (12500, 64), jnp.float32)
        tbl_2 = 0.05 * jax.random.normal(jax.random.fold_in(_tk, 500 + 2), (1000, 64), jnp.float32)
        tbl_3 = 0.05 * jax.random.normal(jax.random.fold_in(_tk, 500 + 3), (12500, 64), jnp.float32)
        tbl_4 = 0.05 * jax.random.normal(jax.random.fold_in(_tk, 500 + 4), (12500, 64), jnp.float32)
        tbl_5 = 0.05 * jax.random.normal(jax.random.fold_in(_tk, 500 + 5), (1000, 64), jnp.float32)
        tbl_6 = 0.05 * jax.random.normal(jax.random.fold_in(_tk, 500 + 6), (12500, 64), jnp.float32)
        tbl_7 = 0.05 * jax.random.normal(jax.random.fold_in(_tk, 500 + 7), (12500, 64), jnp.float32)
        tbl_8 = 0.05 * jax.random.normal(jax.random.fold_in(_tk, 500 + 8), (1250, 64), jnp.float32)
        tbl_9 = 0.05 * jax.random.normal(jax.random.fold_in(_tk, 500 + 9), (12500, 64), jnp.float32)
        tbl_10 = 0.05 * jax.random.normal(jax.random.fold_in(_tk, 500 + 10), (1000, 64), jnp.float32)
        tbl_11 = 0.05 * jax.random.normal(jax.random.fold_in(_tk, 500 + 11), (1000, 64), jnp.float32)
        tbl_12 = 0.05 * jax.random.normal(jax.random.fold_in(_tk, 500 + 12), (1250, 64), jnp.float32)
        tbl_13 = 0.05 * jax.random.normal(jax.random.fold_in(_tk, 500 + 13), (1250, 64), jnp.float32)
        tbl_14 = 0.05 * jax.random.normal(jax.random.fold_in(_tk, 500 + 14), (12500, 64), jnp.float32)
        tbl_15 = 0.05 * jax.random.normal(jax.random.fold_in(_tk, 500 + 15), (12500, 64), jnp.float32)
        tbl_16 = 0.05 * jax.random.normal(jax.random.fold_in(_tk, 500 + 16), (1250, 64), jnp.float32)
        tbl_17 = 0.05 * jax.random.normal(jax.random.fold_in(_tk, 500 + 17), (12500, 64), jnp.float32)
        tbl_18 = 0.05 * jax.random.normal(jax.random.fold_in(_tk, 500 + 18), (12500, 64), jnp.float32)
        tbl_19 = 0.05 * jax.random.normal(jax.random.fold_in(_tk, 500 + 19), (125000, 64), jnp.float32)
        tbl_20 = 0.05 * jax.random.normal(jax.random.fold_in(_tk, 500 + 20), (1250, 64), jnp.float32)
        tbl_21 = 0.05 * jax.random.normal(jax.random.fold_in(_tk, 500 + 21), (1250, 64), jnp.float32)
        tbl_22 = 0.05 * jax.random.normal(jax.random.fold_in(_tk, 500 + 22), (12500, 64), jnp.float32)
        tbl_23 = 0.05 * jax.random.normal(jax.random.fold_in(_tk, 500 + 23), (1000, 64), jnp.float32)
        tbl_24 = 0.05 * jax.random.normal(jax.random.fold_in(_tk, 500 + 24), (12500, 64), jnp.float32)
        tbl_25 = 0.05 * jax.random.normal(jax.random.fold_in(_tk, 500 + 25), (12500, 64), jnp.float32)
        tbl_26 = 0.05 * jax.random.normal(jax.random.fold_in(_tk, 500 + 26), (1000, 64), jnp.float32)
        tbl_27 = 0.05 * jax.random.normal(jax.random.fold_in(_tk, 500 + 27), (1000, 64), jnp.float32)
        tbl_28 = 0.05 * jax.random.normal(jax.random.fold_in(_tk, 500 + 28), (1250, 64), jnp.float32)
        tbl_29 = 0.05 * jax.random.normal(jax.random.fold_in(_tk, 500 + 29), (1250, 64), jnp.float32)
        tbl_30 = 0.05 * jax.random.normal(jax.random.fold_in(_tk, 500 + 30), (1000, 64), jnp.float32)
        tbl_31 = 0.05 * jax.random.normal(jax.random.fold_in(_tk, 500 + 31), (1000, 64), jnp.float32)
        tbl_32 = 0.05 * jax.random.normal(jax.random.fold_in(_tk, 500 + 32), (1000, 64), jnp.float32)
        tbl_33 = 0.05 * jax.random.normal(jax.random.fold_in(_tk, 500 + 33), (12500, 64), jnp.float32)
        tbl_34 = 0.05 * jax.random.normal(jax.random.fold_in(_tk, 500 + 34), (1000, 64), jnp.float32)
        tbl_35 = 0.05 * jax.random.normal(jax.random.fold_in(_tk, 500 + 35), (1250, 64), jnp.float32)
        tbl_36 = 0.05 * jax.random.normal(jax.random.fold_in(_tk, 500 + 36), (1000, 64), jnp.float32)
        tbl_37 = 0.05 * jax.random.normal(jax.random.fold_in(_tk, 500 + 37), (1250, 64), jnp.float32)
        tbl_38 = 0.05 * jax.random.normal(jax.random.fold_in(_tk, 500 + 38), (1000, 64), jnp.float32)
        tbl_39 = 0.05 * jax.random.normal(jax.random.fold_in(_tk, 500 + 39), (1000, 64), jnp.float32)
        _rk = jax.random.fold_in(_tk, 7)
        W_top1 = 0.0354441 * jax.random.normal(jax.random.fold_in(_tk, 801), (796, 512), jnp.float32)
        W_top2 = 0.0441942 * jax.random.normal(jax.random.fold_in(_tk, 802), (512, 256), jnp.float32)
        W_top3 = 0.0625 * jax.random.normal(jax.random.fold_in(_tk, 803), (256, 1), jnp.float32)
        b_top1 = jnp.zeros((512,), jnp.float32)
        b_top2 = jnp.zeros((256,), jnp.float32)
        return (dense_ctx, ids, tbl_0, tbl_1, tbl_2, tbl_3, tbl_4, tbl_5, tbl_6, tbl_7, tbl_8, tbl_9, tbl_10, tbl_11, tbl_12, tbl_13, tbl_14, tbl_15, tbl_16, tbl_17, tbl_18, tbl_19, tbl_20, tbl_21, tbl_22, tbl_23, tbl_24, tbl_25, tbl_26, tbl_27, tbl_28, tbl_29, tbl_30, tbl_31, tbl_32, tbl_33, tbl_34, tbl_35, tbl_36, tbl_37, tbl_38, tbl_39, W_top1, b_top1, W_top2, b_top2, W_top3)
    dense_ctx, ids, tbl_0, tbl_1, tbl_2, tbl_3, tbl_4, tbl_5, tbl_6, tbl_7, tbl_8, tbl_9, tbl_10, tbl_11, tbl_12, tbl_13, tbl_14, tbl_15, tbl_16, tbl_17, tbl_18, tbl_19, tbl_20, tbl_21, tbl_22, tbl_23, tbl_24, tbl_25, tbl_26, tbl_27, tbl_28, tbl_29, tbl_30, tbl_31, tbl_32, tbl_33, tbl_34, tbl_35, tbl_36, tbl_37, tbl_38, tbl_39, W_top1, b_top1, W_top2, b_top2, W_top3 = _rec_inputs()

    def _L0_rec_setup():
        import jax, jax.numpy as jnp
        import numpy as np
        B, N, E = (1024, 40, 64)
        P = N * (N - 1) // 2

        def _pair_indices(n):
            row, col = ([], [])
            for i in range(n - 1):
                for j in range(i + 1, n):
                    row.append(i)
                    col.append(j)
            return (np.asarray(row), np.asarray(col))
        key = jax.random.key(seed)
        k1, k2 = jax.random.split(key)
        inputs = jax.random.normal(k1, (B, N, E), dtype=jnp.float32)
        std = float(np.sqrt(2.0 / (E + E)))
        param = jax.random.normal(k2, (E, P, E), dtype=jnp.float32) * std
        return {'inputs': inputs, 'param': param}
    _L0_rec_all = _L0_rec_setup()
    _L0_rec_in = {k: v for k, v in _L0_rec_all.items() if k in ('param',)}
    del _L0_rec_all
    return {'dense_ctx': dense_ctx, 'ids': ids, 'tbl_0': tbl_0, 'tbl_1': tbl_1, 'tbl_2': tbl_2, 'tbl_3': tbl_3, 'tbl_4': tbl_4, 'tbl_5': tbl_5, 'tbl_6': tbl_6, 'tbl_7': tbl_7, 'tbl_8': tbl_8, 'tbl_9': tbl_9, 'tbl_10': tbl_10, 'tbl_11': tbl_11, 'tbl_12': tbl_12, 'tbl_13': tbl_13, 'tbl_14': tbl_14, 'tbl_15': tbl_15, 'tbl_16': tbl_16, 'tbl_17': tbl_17, 'tbl_18': tbl_18, 'tbl_19': tbl_19, 'tbl_20': tbl_20, 'tbl_21': tbl_21, 'tbl_22': tbl_22, 'tbl_23': tbl_23, 'tbl_24': tbl_24, 'tbl_25': tbl_25, 'tbl_26': tbl_26, 'tbl_27': tbl_27, 'tbl_28': tbl_28, 'tbl_29': tbl_29, 'tbl_30': tbl_30, 'tbl_31': tbl_31, 'tbl_32': tbl_32, 'tbl_33': tbl_33, 'tbl_34': tbl_34, 'tbl_35': tbl_35, 'tbl_36': tbl_36, 'tbl_37': tbl_37, 'tbl_38': tbl_38, 'tbl_39': tbl_39, 'W_top1': W_top1, 'b_top1': b_top1, 'W_top2': W_top2, 'b_top2': b_top2, 'W_top3': W_top3, 'L0_rec_param': _L0_rec_in['param']}

def reference(dense_ctx, ids, tbl_0, tbl_1, tbl_2, tbl_3, tbl_4, tbl_5, tbl_6, tbl_7, tbl_8, tbl_9, tbl_10, tbl_11, tbl_12, tbl_13, tbl_14, tbl_15, tbl_16, tbl_17, tbl_18, tbl_19, tbl_20, tbl_21, tbl_22, tbl_23, tbl_24, tbl_25, tbl_26, tbl_27, tbl_28, tbl_29, tbl_30, tbl_31, tbl_32, tbl_33, tbl_34, tbl_35, tbl_36, tbl_37, tbl_38, tbl_39, W_top1, b_top1, W_top2, b_top2, W_top3, L0_rec_param):
    import jax
    import jax.numpy as jnp

    def _L0_rec_ref(inputs, param):
        import jax, jax.numpy as jnp
        import numpy as np
        B, N, E = (1024, 40, 64)
        P = N * (N - 1) // 2

        def _pair_indices(n):
            row, col = ([], [])
            for i in range(n - 1):
                for j in range(i + 1, n):
                    row.append(i)
                    col.append(j)
            return (np.asarray(row), np.asarray(col))
        n = inputs.shape[1]
        rowidx, colidx = _pair_indices(n)
        p = inputs[:, rowidx]
        q = inputs[:, colidx]
        out = jnp.einsum('bie,fie,bif->bi', p, param, q)
        return out[:, None, :]
    e = jnp.stack([tbl_0[ids[:, 0]], tbl_1[ids[:, 1]], tbl_2[ids[:, 2]], tbl_3[ids[:, 3]], tbl_4[ids[:, 4]], tbl_5[ids[:, 5]], tbl_6[ids[:, 6]], tbl_7[ids[:, 7]], tbl_8[ids[:, 8]], tbl_9[ids[:, 9]], tbl_10[ids[:, 10]], tbl_11[ids[:, 11]], tbl_12[ids[:, 12]], tbl_13[ids[:, 13]], tbl_14[ids[:, 14]], tbl_15[ids[:, 15]], tbl_16[ids[:, 16]], tbl_17[ids[:, 17]], tbl_18[ids[:, 18]], tbl_19[ids[:, 19]], tbl_20[ids[:, 20]], tbl_21[ids[:, 21]], tbl_22[ids[:, 22]], tbl_23[ids[:, 23]], tbl_24[ids[:, 24]], tbl_25[ids[:, 25]], tbl_26[ids[:, 26]], tbl_27[ids[:, 27]], tbl_28[ids[:, 28]], tbl_29[ids[:, 29]], tbl_30[ids[:, 30]], tbl_31[ids[:, 31]], tbl_32[ids[:, 32]], tbl_33[ids[:, 33]], tbl_34[ids[:, 34]], tbl_35[ids[:, 35]], tbl_36[ids[:, 36]], tbl_37[ids[:, 37]], tbl_38[ids[:, 38]], tbl_39[ids[:, 39]]], axis=1)
    z = _L0_rec_ref(e, L0_rec_param)
    z = z.reshape(z.shape[0], -1)
    h = jnp.concatenate([z, dense_ctx], axis=1)
    h = jnp.maximum(h @ W_top1 + b_top1, 0.0)
    h = jnp.maximum(h @ W_top2 + b_top2, 0.0)
    y = h @ W_top3
    return y

_drawn_inputs = setup_inputs


def setup_inputs(seed=0):
    import zlib

    import numpy as np

    out = dict(_drawn_inputs(seed))
    spreads = {'b_top1': (0.0, 0.1), 'b_top2': (0.0, 0.1)}
    factors = {}
    for name, (base, spread) in spreads.items():
        noise = np.random.default_rng([zlib.crc32(name.encode()), seed]).standard_normal(out[name].shape)
        drawn = base * np.exp(spread * noise) if base else spread * noise
        out[name] = jnp.asarray(drawn.astype(out[name].dtype))
    for name, factor in factors.items():
        out[name] = (out[name] * factor).astype(out[name].dtype)
    return out
```

```python
from contextlib import ExitStack

import concourse.bass as bass
from concourse import mybir

F32 = mybir.dt.float32
F32R = mybir.dt.float32r
I32 = mybir.dt.int32
ALU = mybir.AluOpType
ACT = mybir.ActivationFunctionType

P = 128
FIELDS, E = 40, 64
HALVES = 2
COUPLES = FIELDS // 2
STEPS = COUPLES
CHUNK = 512
QRING, STAGES, WRING, PRING = 6, 8, 4, 2
GATHER_LEAD = STAGES - 1
W_LEAD = 2


def pair_index(i, j):
    return i * (2 * FIELDS - 1 - i) // 2 + (j - i - 1)


def plan_units():
    units = []
    for J in range(STEPS - 1):
        units += [(J, [(m, 2 * J + 1), (m, 2 * J + 2)]) for m in range(J + 1)]
    last = STEPS - 1
    units += [(last, [(m + 1, FIELDS - 1), (m, FIELDS - 1)]) for m in range(COUPLES - 2, -1, -2)]
    return units


def tower_kernel(nc, dense_ctx, ids, tables, W_top1, b_top1, W_top2, b_top2, W_top3, param, out):
    B, CTX = dense_ctx.shape
    H1, H2 = W_top1.shape[1], W_top2.shape[1]
    PAIRS = param.shape[1]
    HB = B // HALVES
    BLOCKS = HB // P
    CHUNKS = HB // CHUNK
    M1, M2 = H1 // P, H2 // P

    UNITS = plan_units()
    NU = len(UNITS)
    NT = 2 * NU
    UPG = 32
    GROUPS = -(-NU // UPG)
    first_of_step = {}
    units_of_step = {}
    for u, (J, _) in enumerate(UNITS):
        first_of_step.setdefault(J, u)
        units_of_step[J] = units_of_step.get(J, 0) + 1
    last_tile_of_q = {}
    for u, (_, tiles) in enumerate(UNITS):
        for t, (m, j) in enumerate(tiles):
            last_tile_of_q[j] = 2 * u + t

    def is_single(m, j):
        return 2 * m + 1 == j

    FIRST_COUPLES = [0, 1]
    turn_in = {first_of_step[J] + max(0, units_of_step[J] - 4): J + 2 for J in range(STEPS - 2)}

    def q_order(h, k):
        return h * (FIELDS - 1) + max(k - 1, 0)

    def q_fields(F):
        return [k for k in (2 * F, 2 * F + 1) if k]

    DVE_SPLITS = first_of_step[8]

    ctx = ExitStack()
    with ctx:
        def sb(name, shape, dt=F32):
            return ctx.enter_context(nc.sbuf_tensor(name, shape, dt))

        def psum(name, shape):
            return ctx.enter_context(nc.psum_tensor(name, shape, F32))

        def sem(name):
            return ctx.enter_context(nc.semaphore(name))

        idx = sb("idx", [P, B // P, FIELDS], I32)
        stage = sb("stage", [P, STAGES, BLOCKS, 2, E])
        pT = sb("pT", [P, COUPLES, HB])
        q = sb("q", [P, QRING, HB], F32R)
        w_raw = sb("w_raw", [P, WRING, 4 * E])
        w_split = sb("w_split", [P, WRING, 2, 4 * E], F32R)
        prod = sb("prod", [P, PRING, 2, HB])
        zs = sb("zs", [P, GROUPS, HB])
        sel = sb("sel", [P, 62])
        sel_single = sb("sel_single", [P, 62])
        ident = sb("ident", [P, P])
        ctx_rows = sb("ctx_rows", [P, B // P, 32])
        zeros = sb("zeros", [32, H1])
        b1 = sb("b1", [P, M1])
        b2 = sb("b2", [P, M2])
        w3 = sb("w3", [P, M2])
        MLP_COUPLE = 8
        y_sb = pT[0:1, 8, :]
        h2 = pT[:, 9:11, :]
        h1 = pT[:, 11:15, :]
        w2 = pT[:, 15, 0:M1 * H2].rearrange("p (k n) -> p k n", n=H2)
        w1 = pT[:, 16:20, :].rearrange("p a b -> p (a b)")[:, 0:GROUPS * H1].rearrange(
            "p (g n) -> p g n", n=H1)
        w1_rows = nc.dram_tensor("w1_rows", [GROUPS * P, H1], F32, kind="Internal").ap()

        T = [psum(f"T{i}", [P, HB]) for i in range(2)]
        turn = psum("turn", [P, HB])
        z = psum("z", [P, CHUNKS, CHUNK])

        ids_in = sem("ids_in")
        consts_in = sem("consts_in")
        consts_made = sem("consts_made")
        zeroed = sem("zeroed")
        ident_made = sem("ident_made")
        gathered = [sem(f"gathered{i}") for i in range(STAGES)]
        turned = sem("turned")
        p_ready = sem("p_ready")
        q_hi_ready = sem("q_hi_ready")
        q_lo_ready = sem("q_lo_ready")
        w_in = [sem(f"w_in{i}") for i in range(WRING)]
        w_hi_ready = sem("w_hi_ready")
        w_lo_dve = sem("w_lo_dve")
        w_lo_pool = sem("w_lo_pool")
        T_ready = sem("T_ready")
        prod_ready = sem("prod_ready")
        summed = sem("summed")
        z_out = sem("z_out")
        w1_placed = sem("w1_placed")
        tower_in = sem("tower_in")
        layer_done = sem("layer_done")
        layer_out = sem("layer_out")
        y_out = sem("y_out")

        block = ctx.enter_context(nc.Block())

        TOWER_BLOCKS = CHUNKS * (M1 + M2 + 1)
        W1_DMAS = (STEPS - 1) * STEPS // 2 + COUPLES + 1 + 4

        def wait_w_lo(eng, U):
            if U < DVE_SPLITS:
                eng.wait_ge(w_lo_dve, U + 1)
            else:
                eng.wait_ge(w_lo_pool, U - DVE_SPLITS + 1)

        w_counts = {}
        total = [0] * WRING
        for U in range(HALVES * NU):
            total[U % WRING] += 32 if UNITS[U % NU][0] < STEPS - 1 else 64
            w_counts[U] = total[U % WRING]

        def as_loaded(ap, J):
            return ap if J == STEPS - 1 else ap.rearrange("p (i j e) -> p i j e", j=2, i=2)

        def as_split(ap, J):
            return ap if J == STEPS - 1 else ap.rearrange("p (j i e) -> p i j e", j=2, i=2)

        @block.sync
        def _(sp):
            sp.dma_start(idx[:, :, :], ids.rearrange("(c p) f -> p c f", p=P)).then_inc(ids_in, 16)

            def load_weights(U):
                J, tiles = UNITS[U % NU]
                s = U % WRING
                if U >= WRING:
                    wait_w_lo(sp, U - WRING)
                for half in (0, E):
                    dst = w_raw[half:half + E, s, :]
                    if J < STEPS - 1:
                        m = tiles[0][0]
                        at, step = pair_index(2 * m, 2 * J + 1), FIELDS - 2 - 2 * m
                        src = bass.AP(param.tensor, at * E,
                                      [[PAIRS * E, E], [step * E, 2], [1, 2 * E]])
                        sp.dma_start(dst.rearrange("p (i x) -> p i x", i=2), src).then_inc(w_in[s], 16)
                    else:
                        for t, (m, j) in enumerate(tiles):
                            at, step = pair_index(2 * m, j), FIELDS - 2 - 2 * m
                            src = bass.AP(param.tensor, at * E,
                                          [[PAIRS * E, E], [step * E, 2], [1, E]])
                            sp.dma_start(dst[:, 2 * E * t:2 * E * (t + 1)].rearrange(
                                "p (i e) -> p i e", i=2), src).then_inc(w_in[s], 16)

            def place_w1(u):
                J, tiles = UNITS[u]
                g, v = divmod(u, UPG)
                s, par = divmod(v, 2)
                row = g * P + 64 * par + 2 * s
                if J < STEPS - 1:
                    m = tiles[0][0]
                    step = FIELDS - 2 - 2 * m
                    src = bass.AP(W_top1.tensor, pair_index(2 * m, 2 * J + 1) * H1,
                                  [[H1, 2], [step * H1, 2], [1, H1]])
                    dst = bass.AP(w1_rows.tensor, row * H1, [[32 * H1, 2], [H1, 2], [1, H1]])
                    sp.dma_start(dst, src).then_inc(w1_placed, 16)
                else:
                    for t, (m, j) in enumerate(tiles):
                        step = FIELDS - 2 - 2 * m
                        src = bass.AP(W_top1.tensor, pair_index(2 * m, j) * H1, [[step * H1, 2], [1, H1]])
                        sp.dma_start(w1_rows[row + 32 * t:row + 32 * t + 2, :], src).then_inc(w1_placed, 16)

            for h in range(HALVES):
                for u in range(NU):
                    load_weights(h * NU + u)
                    if h == 0:
                        place_w1(u)
                        if u == WRING:
                            base = (GROUPS - 1) * P
                            used = NU % UPG
                            sp.dma_start(w1_rows[base + used:base + used + CTX, :],
                                         W_top1[PAIRS:PAIRS + CTX, :]).then_inc(w1_placed, 16)
                            sp.wait_ge(zeroed, 1)
                            for quad in range(4):
                                a = base + 32 * quad + used + (CTX if quad == 0 else 0)
                                n = base + 32 * (quad + 1) - a
                                sp.dma_start(w1_rows[a:a + n, :], zeros[0:n, :]).then_inc(w1_placed, 16)
                if h == 0:
                    sp.wait_ge(w1_placed, 16 * W1_DMAS)
                sp.wait_ge(prod_ready, h * NT + NT - 20 + 6)
                sp.dma_start(w1, w1_rows.rearrange("(g p) n -> p g n", p=P)).then_inc(tower_in, 16)
                sp.dma_start(w2, W_top2.rearrange("(k p) n -> p k n", p=P)).then_inc(tower_in, 16)
                sp.wait_ge(layer_out, TOWER_BLOCKS * (h + 1))
                sp.dma_start(out[h * HB:(h + 1) * HB, :].rearrange("b o -> o b"), y_sb).then_inc(y_out, 16)
            sp.wait_ge(y_out, 16 * HALVES)

        @block.gpsimd
        def _(pool):
            pool.wait_ge(ids_in, 16)

            def gather(a, n):
                h, F = divmod(a, COUPLES)
                c, x = divmod(n, 2)
                if a >= STAGES and n == 0:
                    pool.wait_ge(turned, a - STAGES + 1)
                pool.indirect_dma_start(
                    out=stage[:, a % STAGES, c, x, :], out_offset=None, in_=tables[2 * F + x][:, :],
                    in_offset=bass.IndirectOffsetOnAxis(ap=idx[:, h * BLOCKS + c, 2 * F + x:2 * F + x + 1], axis=0),
                ).then_inc(gathered[a % STAGES], 16)

            def split_lo(U):
                J = UNITS[U % NU][0]
                s = U % WRING
                pool.wait_ge(w_hi_ready, U + 1)
                pool.tensor_tensor(as_split(w_split[:, s, 1, :], J), as_loaded(w_raw[:, s, :], J),
                                   as_split(w_split[:, s, 0, :], J).bitcast(F32), ALU.subtract).then_inc(w_lo_pool, 1)

            for n in range(2 * BLOCKS):
                gather(0, n)
            pool.wait_ge(ident_made, 1)
            pool.affine_select(out=ident[:, :], in_=ident[:, :], compare_op=ALU.not_equal, fill=1.0,
                               base=0, pattern=[[-1, P]], channel_multiplier=1).then_inc(ident_made, 1)
            for a in range(1, GATHER_LEAD):
                for n in range(2 * BLOCKS):
                    gather(a, n)
            for h in range(HALVES):
                if h * NU >= DVE_SPLITS:
                    for U in range(h * NU, h * NU + W_LEAD):
                        split_lo(U)
                for u, (J, _) in enumerate(UNITS):
                    a = h * COUPLES + J + GATHER_LEAD
                    n, k = units_of_step[J], u - first_of_step[J]
                    if a < HALVES * COUPLES:
                        for x in range(2 * BLOCKS * k // n, 2 * BLOCKS * (k + 1) // n):
                            gather(a, x)
                    if u + W_LEAD < NU and h * NU + u + W_LEAD >= DVE_SPLITS:
                        split_lo(h * NU + u + W_LEAD)

        @block.scalar
        def _(act):
            with nc.allow_non_contiguous_dma(reason="biases and the last layer, 1024 values"):
                act.dma_start(b1[:, :], b_top1.rearrange("(m p) -> p m", p=P)).then_inc(consts_in, 16)
                act.dma_start(b2[:, :], b_top2.rearrange("(m p) -> p m", p=P)).then_inc(consts_in, 16)
                act.dma_start(w3[:, :], W_top3.rearrange("(m p) o -> p (m o)", p=P)).then_inc(consts_in, 16)
            act.wait_ge(zeroed, 4)
            used = NU % UPG
            act.dma_start(ctx_rows[:, :, used:used + CTX],
                          dense_ctx.rearrange("(c p) x -> p c x", p=P)).then_inc(consts_in, 16)

            def split_hi(U):
                J = UNITS[U % NU][0]
                s = U % WRING
                act.wait_ge(w_in[s], w_counts[U])
                if U >= WRING:
                    act.wait_ge(T_ready, 2 * (U - WRING) + 2)
                act.copy(as_split(w_split[:, s, 0, :], J), as_loaded(w_raw[:, s, :], J)).then_inc(w_hi_ready, 1)

            def take_couple(h, F):
                act.wait_ge(turned, h * COUPLES + F + 1)
                if h and F == 0:
                    act.wait_ge(prod_ready, h * NT)
                if h and F == MLP_COUPLE:
                    act.wait_ge(y_out, 16 * h)
                act.copy(pT[:, F, :], turn[:, :]).then_inc(p_ready, 1)
                for k in q_fields(F):
                    Q, side = q_order(h, k), E * (k % 2)
                    if Q >= QRING:
                        hh, kk = divmod(Q - QRING, FIELDS - 1)
                        act.wait_ge(T_ready, hh * NT + last_tile_of_q[kk + 1] + 1)
                    act.copy(q[side:side + E, Q % QRING, :], turn[side:side + E, :]).then_inc(q_hi_ready, 1)

            def take_z(h, g):
                G = h * GROUPS + g
                act.wait_ge(summed, h * NU + min(UPG * (g + 1), NU))
                if h:
                    act.wait_ge(layer_done, TOWER_BLOCKS * h)
                act.copy(zs[:, g, 0:CHUNK], z[:, 0, :]).then_inc(z_out, 1)
                act.copy(zs[0:64, g, CHUNK:HB], z[64:P, 1, :]).then_inc(z_out, 1)
                act.copy(zs[64:P, g, CHUNK:HB], z[0:64, 1, :]).then_inc(z_out, 1)

            def tower(h):
                n = TOWER_BLOCKS * h

                def step(f):
                    nonlocal n
                    act.wait_ge(layer_done, n + 1)
                    f(turn[:, CHUNK * (n % 2):CHUNK * (n % 2 + 1)]).then_inc(layer_out, 1)
                    n += 1

                if h == 0:
                    act.wait_ge(consts_in, 64)
                for c in range(CHUNKS):
                    cols = slice(CHUNK * c, CHUNK * (c + 1))
                    for m in range(M1):
                        step(lambda t: act.activation(h1[:, m, cols], t, ACT.Relu, bias=b1[:, m:m + 1]))
                for c in range(CHUNKS):
                    cols = slice(CHUNK * c, CHUNK * (c + 1))
                    for m in range(M2):
                        step(lambda t: act.activation(h2[:, m, cols], t, ACT.Relu, bias=b2[:, m:m + 1]))
                for c in range(CHUNKS):
                    cols = slice(CHUNK * c, CHUNK * (c + 1))
                    step(lambda t: act.copy(y_sb[:, cols], t[0:1, :]))

            for h in range(HALVES):
                for U in range(h * NU, h * NU + W_LEAD):
                    split_hi(U)
                if h == 0:
                    for F in FIRST_COUPLES:
                        take_couple(h, F)
                for u in range(NU):
                    if u + W_LEAD < NU:
                        split_hi(h * NU + u + W_LEAD)
                    if u and u % UPG == 0:
                        take_z(h, u // UPG - 1)
                    if u in turn_in:
                        take_couple(h, turn_in[u])
                take_z(h, GROUPS - 1)
                if h + 1 < HALVES:
                    for F in FIRST_COUPLES:
                        take_couple(h + 1, F)
                tower(h)

        @block.vector
        def _(dve):
            def split_lo(U):
                J = UNITS[U % NU][0]
                s = U % WRING
                dve.wait_ge(w_hi_ready, U + 1)
                dve.tensor_tensor(as_split(w_split[:, s, 1, :], J), as_loaded(w_raw[:, s, :], J),
                                  as_split(w_split[:, s, 0, :], J).bitcast(F32), ALU.subtract).then_inc(w_lo_dve, 1)

            def q_lo(h, F):
                for k in q_fields(F):
                    Q, side, other = q_order(h, k), E * (k % 2), E * (1 - k % 2)
                    dve.wait_ge(q_hi_ready, Q + 1)
                    dve.tensor_tensor(q[other:other + E, Q % QRING, :], turn[side:side + E, :],
                                      q[side:side + E, Q % QRING, :].bitcast(F32),
                                      ALU.subtract).then_inc(q_lo_ready, 1)

            def products(h, u):
                U = h * NU + u
                for t, (m, j) in enumerate(UNITS[u][1]):
                    tile = 2 * U + t
                    dve.wait_ge(T_ready, tile + 1)
                    dve.wait_ge(p_ready, h * COUPLES + m + 1)
                    if U >= PRING:
                        dve.wait_ge(summed, U - PRING + 1)
                    dve.tensor_tensor(prod[:, U % PRING, t, :], T[t][:, :], pT[:, m, :],
                                      ALU.mult).then_inc(prod_ready, 1)

            dve.memset(ident[:, :], 0.0).then_inc(ident_made, 1)
            dve.memset(zeros[:, :], 0.0).then_inc(zeroed, 1)
            dve.memset(ctx_rows[:, :, :], 0.0).then_inc(zeroed, 1)
            dve.memset(sel[:, :], 0.0).then_inc(zeroed, 1)
            dve.memset(sel_single[:, :], 0.0).then_inc(zeroed, 1)
            dve.wait_ge(zeroed, 4)
            dve.memset(sel[0:E, 30:31], 1.0).then_inc(consts_made, 1)
            dve.memset(sel[E:P, 31:32], 1.0).then_inc(consts_made, 1)
            dve.memset(sel_single[0:E, 30:31], 1.0).then_inc(consts_made, 1)
            for h in range(HALVES):
                if h == 0:
                    for U in range(W_LEAD):
                        split_lo(U)
                    for F in FIRST_COUPLES:
                        q_lo(h, F)
                for u in range(NU):
                    products(h, u)
                    if h == 0 and u + W_LEAD < DVE_SPLITS:
                        split_lo(u + W_LEAD)
                    if u in turn_in:
                        q_lo(h, turn_in[u])
                if h + 1 < HALVES:
                    for F in FIRST_COUPLES:
                        q_lo(h + 1, F)

        @block.tensor
        def _(pe):
            def turn_free(h, F):
                pe.wait_ge(p_ready, h * COUPLES + F)
                pe.wait_ge(q_lo_ready, q_order(h, 2 * F))

            def turn_couple(h, F):
                a = h * COUPLES + F
                if a:
                    turn_free(h, F)
                if h and F == len(FIRST_COUPLES):
                    pe.wait_ge(layer_out, TOWER_BLOCKS * h)
                pe.wait_ge(gathered[a % STAGES], 16 * 2 * BLOCKS * (a // STAGES + 1))
                for c in range(BLOCKS):
                    mm = pe.transpose(turn[:, P * c:P * (c + 1)],
                                      stage[:, a % STAGES, c, :, :].rearrange("p x e -> p (x e)"), ident[:, :])
                mm.then_inc(turned, 1)

            def bilinear(h, u):
                U = h * NU + u
                wait_w_lo(pe, U)
                for t, (m, j) in enumerate(UNITS[u][1]):
                    tile = 2 * U + t
                    Q = q_order(h, j)
                    pe.wait_ge(q_lo_ready, Q + 1)
                    if tile >= 2:
                        pe.wait_ge(prod_ready, tile - 1)
                    for c in range(CHUNKS):
                        for part in (0, 1):
                            mm = pe.matmul(T[t][:, CHUNK * c:CHUNK * (c + 1)],
                                           w_split[:, U % WRING, part, P * t:P * (t + 1)],
                                           q[:, Q % QRING, CHUNK * c:CHUNK * (c + 1)],
                                           start=(part == 0), stop=(part == 1))
                    mm.then_inc(T_ready, 1)

            def reduce(h, u):
                U = h * NU + u
                g, v = divmod(u, UPG)
                s, par = divmod(v, 2)
                in_group = min(UPG, NU - g * UPG)
                pe.wait_ge(prod_ready, 2 * U + 2)
                if v == 0 and (h or g):
                    pe.wait_ge(z_out, 3 * (h * GROUPS + g))
                for c in range(CHUNKS):
                    for t, (m, j) in enumerate(UNITS[u][1]):
                        quad = 2 * (par if c == 0 else 1 - par) + t
                        pick = sel_single if is_single(m, j) else sel
                        mm = pe.matmul(z[32 * quad:32 * quad + 32, c, :], pick[:, 30 - 2 * s:62 - 2 * s],
                                       prod[:, U % PRING, t, CHUNK * c:CHUNK * (c + 1)],
                                       start=(v < 2), stop=(v + 2 >= in_group))
                mm.then_inc(summed, 1)

            def add_ctx(h):
                if h == 0:
                    pe.wait_ge(consts_in, 64)
                for c in range(BLOCKS):
                    chunk, at = divmod(P * c, CHUNK)
                    quad = 0 if chunk == 0 else 2
                    pe.matmul(z[32 * quad:32 * quad + 32, chunk, at:at + P],
                              ctx_rows[:, h * BLOCKS + c, :], ident[:, :], start=False, stop=False)

            def tower(h):
                n = TOWER_BLOCKS * h
                pe.wait_ge(tower_in, 32 * (h + 1))
                if h + 1 < HALVES:
                    turn_free(h + 1, len(FIRST_COUPLES))
                else:
                    turn_free(h, COUPLES)

                def block_of(M, parts):
                    nonlocal n
                    if n >= TOWER_BLOCKS * h + 2:
                        pe.wait_ge(layer_out, n - 1)
                    for i, (w, x) in enumerate(parts):
                        mm = pe.matmul(turn[0:M, CHUNK * (n % 2):CHUNK * (n % 2 + 1)], w, x,
                                       start=(i == 0), stop=(i == len(parts) - 1))
                    mm.then_inc(layer_done, 1)
                    n += 1

                pe.wait_ge(z_out, 3 * GROUPS * (h + 1))
                for c in range(CHUNKS):
                    cols = slice(CHUNK * c, CHUNK * (c + 1))
                    for m in range(M1):
                        block_of(P, [(w1[:, g, P * m:P * (m + 1)], zs[:, g, cols]) for g in range(GROUPS)])
                pe.wait_ge(layer_out, TOWER_BLOCKS * h + CHUNKS * M1)
                for c in range(CHUNKS):
                    cols = slice(CHUNK * c, CHUNK * (c + 1))
                    for m in range(M2):
                        block_of(P, [(w2[:, k, P * m:P * (m + 1)], h1[:, k, cols]) for k in range(M1)])
                pe.wait_ge(layer_out, TOWER_BLOCKS * h + CHUNKS * (M1 + M2))
                for c in range(CHUNKS):
                    cols = slice(CHUNK * c, CHUNK * (c + 1))
                    block_of(1, [(w3[:, k:k + 1], h2[:, k, cols]) for k in range(M2)])

            pe.wait_ge(ident_made, 2)
            pe.wait_ge(consts_made, 3)
            for h in range(HALVES):
                if h == 0:
                    for F in FIRST_COUPLES:
                        turn_couple(h, F)
                for u in range(NU):
                    bilinear(h, u)
                    if u:
                        reduce(h, u - 1)
                    if u - 1 == (GROUPS - 1) * UPG + 1:
                        add_ctx(h)
                    if u in turn_in:
                        turn_couple(h, turn_in[u])
                reduce(h, NU - 1)
                if h + 1 < HALVES:
                    for F in FIRST_COUPLES:
                        turn_couple(h + 1, F)
                tower(h)


def kernel(**inputs):
    import numpy as np
    from concourse import bacc
    from concourse.bass_utils import run_bass_kernel_spmd

    names = (["dense_ctx", "ids"] + [f"tbl_{f}" for f in range(FIELDS)]
             + ["W_top1", "b_top1", "W_top2", "b_top2", "W_top3", "L0_rec_param"])
    nc = bacc.Bacc("TRN2", target_bir_lowering=False, num_devices=1)
    arrays, aps = {}, {}
    for name in names:
        a = np.ascontiguousarray(inputs[name])
        arrays[f"in_{name}"] = a
        aps[name] = nc.dram_tensor(f"in_{name}", a.shape, mybir.dt.from_np(a.dtype), kind="ExternalInput").ap()
    B = inputs["dense_ctx"].shape[0]
    out = nc.dram_tensor("out_y", (B, 1), F32, kind="ExternalOutput").ap()
    tower_kernel(nc, aps["dense_ctx"], aps["ids"], [aps[f"tbl_{f}"] for f in range(FIELDS)],
                 aps["W_top1"], aps["b_top1"], aps["W_top2"], aps["b_top2"], aps["W_top3"],
                 aps["L0_rec_param"], out)
    r = run_bass_kernel_spmd(nc, [arrays], core_ids=[0])
    return r.results[0]["out_y"]
```

```python
from contextlib import ExitStack

import concourse.bass as bass
from concourse import mybir

F32 = mybir.dt.float32
F32R = mybir.dt.float32r
I32 = mybir.dt.int32
ALU = mybir.AluOpType
ACT = mybir.ActivationFunctionType

P = 128
FIELDS, E = 40, 64
HALVES = 2
COUPLES = FIELDS // 2
STEPS = COUPLES
CHUNK = 512
QRING, STAGES, WRING, PRING = 8, 6, 3, 3
GATHER_LEAD = STAGES - 1
SUM_LAG = 2
W_LEAD = 2


def pair_index(i, j):
    return i * (2 * FIELDS - 1 - i) // 2 + (j - i - 1)


def plan_units():
    units = []
    for J in range(STEPS - 1):
        units += [(J, [(m, 2 * J + 1), (m, 2 * J + 2)]) for m in range(J + 1)]
    last = STEPS - 1
    units += [(last, [(m + 1, FIELDS - 1), (m, FIELDS - 1)]) for m in range(COUPLES - 2, -1, -2)]
    return units


def tower_kernel(nc, dense_ctx, ids, tables, W_top1, b_top1, W_top2, b_top2, W_top3, param, out):
    B, CTX = dense_ctx.shape
    H1, H2 = W_top1.shape[1], W_top2.shape[1]
    PAIRS = param.shape[1]
    HB = B // HALVES
    BLOCKS = HB // P
    CHUNKS = HB // CHUNK
    M1, M2 = H1 // P, H2 // P

    UNITS = plan_units()
    NU = len(UNITS)
    NT = 2 * NU
    UPG = 32
    GROUPS = -(-NU // UPG)
    first_of_step = {}
    units_of_step = {}
    for u, (J, _) in enumerate(UNITS):
        first_of_step.setdefault(J, u)
        units_of_step[J] = units_of_step.get(J, 0) + 1
    last_tile_of_q = {}
    for u, (_, tiles) in enumerate(UNITS):
        for t, (m, j) in enumerate(tiles):
            last_tile_of_q[j] = 2 * u + t

    def is_single(m, j):
        return 2 * m + 1 == j

    FIRST_COUPLES = [range(2), range(3)]
    turn_in = [{}, {}]
    for J in range(STEPS - 2):
        n = units_of_step[J]
        turn_in[0][first_of_step[J] + (n - 1 if J < 8 else n - 5)] = J + 2
    for J in range(STEPS - 3):
        turn_in[1][first_of_step[J]] = J + 3
    q_lo_in = [{}, {}]
    for h in range(HALVES):
        for u, F in turn_in[h].items():
            J, room = UNITS[u][0], first_of_step[UNITS[u][0]] + units_of_step[UNITS[u][0]] - 1
            for x in (0, 1):
                q_lo_in[h].setdefault(min(u + 1 + x, room + h), []).append(2 * F + x)

    def q_order(h, k):
        return h * (FIELDS - 1) + max(k - 1, 0)

    def q_fields(F):
        return [k for k in (2 * F, 2 * F + 1) if k]

    DVE_SPLITS = [u < first_of_step[14] for u in range(NU)] + [u < first_of_step[7] for u in range(NU)]

    ctx = ExitStack()
    with ctx:
        def sb(name, shape, dt=F32):
            return ctx.enter_context(nc.sbuf_tensor(name, shape, dt))

        def psum(name, shape):
            return ctx.enter_context(nc.psum_tensor(name, shape, F32))

        def sem(name):
            return ctx.enter_context(nc.semaphore(name))

        idx = sb("idx", [P, B // P, FIELDS], I32)
        stage = sb("stage", [P, STAGES, BLOCKS, 2, E])
        pT = sb("pT", [P, COUPLES, HB])
        q = sb("q", [P, QRING, HB], F32R)
        w_raw = sb("w_raw", [P, WRING, 4 * E])
        w_split = sb("w_split", [P, WRING, 2, 4 * E], F32R)
        prod = sb("prod", [P, PRING, 2, HB])
        zs = sb("zs", [P, GROUPS, HB])
        sel = sb("sel", [P, 62])
        sel_single = sb("sel_single", [P, 62])
        ident = sb("ident", [P, P])
        ctx_rows = sb("ctx_rows", [P, B // P, 32])
        zeros = sb("zeros", [32, H1])
        b1 = sb("b1", [P, M1])
        b2 = sb("b2", [P, M2])
        w3 = sb("w3", [P, M2])
        MLP_COUPLE = 8
        y_sb = pT[0:1, 8, :]
        h2 = pT[:, 9:11, :]
        h1 = pT[:, 11:15, :]
        w2 = pT[:, 15, 0:M1 * H2].rearrange("p (k n) -> p k n", n=H2)
        w1 = pT[:, 16:20, :].rearrange("p a b -> p (a b)")[:, 0:GROUPS * H1].rearrange(
            "p (g n) -> p g n", n=H1)
        w1_rows = nc.dram_tensor("w1_rows", [GROUPS * P, H1], F32, kind="Internal").ap()

        T = [psum(f"T{i}", [P, HB]) for i in range(2)]
        turn = psum("turn", [P, HB])
        z = psum("z", [P, CHUNKS, CHUNK])

        ids_in = sem("ids_in")
        consts_in = sem("consts_in")
        consts_made = sem("consts_made")
        zeroed = sem("zeroed")
        ident_made = sem("ident_made")
        gathered = [sem(f"gathered{i}") for i in range(STAGES)]
        turned = sem("turned")
        p_ready = sem("p_ready")
        q_hi_ready = sem("q_hi_ready")
        q_lo_ready = sem("q_lo_ready")
        w_in = [sem(f"w_in{i}") for i in range(WRING)]
        w_hi_ready = sem("w_hi_ready")
        w_lo_dve = sem("w_lo_dve")
        w_lo_pool = sem("w_lo_pool")
        T_ready = sem("T_ready")
        prod_ready = sem("prod_ready")
        summed = sem("summed")
        z_out = sem("z_out")
        w1_placed = sem("w1_placed")
        tower_in = sem("tower_in")
        layer_done = sem("layer_done")
        layer_out = sem("layer_out")
        y_out = sem("y_out")

        block = ctx.enter_context(nc.Block())

        TOWER_BLOCKS = CHUNKS * (M1 + M2 + 1)
        W1_DMAS = (STEPS - 1) * STEPS // 2 + COUPLES + 1 + 4

        def wait_w_lo(eng, U):
            n = sum(DVE_SPLITS[:U + 1])
            if DVE_SPLITS[U]:
                eng.wait_ge(w_lo_dve, n)
            else:
                eng.wait_ge(w_lo_pool, U + 1 - n)

        w_counts = {}
        total = [0] * WRING
        for U in range(HALVES * NU):
            total[U % WRING] += 32 if UNITS[U % NU][0] < STEPS - 1 else 64
            w_counts[U] = total[U % WRING]

        def as_loaded(ap, J):
            return ap if J == STEPS - 1 else ap.rearrange("p (i j e) -> p i j e", j=2, i=2)

        def as_split(ap, J):
            return ap if J == STEPS - 1 else ap.rearrange("p (j i e) -> p i j e", j=2, i=2)

        @block.sync
        def _(sp):
            sp.dma_start(idx[:, :, :], ids.rearrange("(c p) f -> p c f", p=P)).then_inc(ids_in, 16)

            def load_weights(U):
                J, tiles = UNITS[U % NU]
                s = U % WRING
                if U >= WRING:
                    wait_w_lo(sp, U - WRING)
                for half in (0, E):
                    dst = w_raw[half:half + E, s, :]
                    if J < STEPS - 1:
                        m = tiles[0][0]
                        at, step = pair_index(2 * m, 2 * J + 1), FIELDS - 2 - 2 * m
                        src = bass.AP(param.tensor, at * E,
                                      [[PAIRS * E, E], [step * E, 2], [1, 2 * E]])
                        sp.dma_start(dst.rearrange("p (i x) -> p i x", i=2), src).then_inc(w_in[s], 16)
                    else:
                        for t, (m, j) in enumerate(tiles):
                            at, step = pair_index(2 * m, j), FIELDS - 2 - 2 * m
                            src = bass.AP(param.tensor, at * E,
                                          [[PAIRS * E, E], [step * E, 2], [1, E]])
                            sp.dma_start(dst[:, 2 * E * t:2 * E * (t + 1)].rearrange(
                                "p (i e) -> p i e", i=2), src).then_inc(w_in[s], 16)

            def place_w1(u):
                J, tiles = UNITS[u]
                g, v = divmod(u, UPG)
                s, par = divmod(v, 2)
                row = g * P + 64 * par + 2 * s
                if J < STEPS - 1:
                    m = tiles[0][0]
                    step = FIELDS - 2 - 2 * m
                    src = bass.AP(W_top1.tensor, pair_index(2 * m, 2 * J + 1) * H1,
                                  [[H1, 2], [step * H1, 2], [1, H1]])
                    dst = bass.AP(w1_rows.tensor, row * H1, [[32 * H1, 2], [H1, 2], [1, H1]])
                    sp.dma_start(dst, src).then_inc(w1_placed, 16)
                else:
                    for t, (m, j) in enumerate(tiles):
                        step = FIELDS - 2 - 2 * m
                        src = bass.AP(W_top1.tensor, pair_index(2 * m, j) * H1, [[step * H1, 2], [1, H1]])
                        sp.dma_start(w1_rows[row + 32 * t:row + 32 * t + 2, :], src).then_inc(w1_placed, 16)

            for h in range(HALVES):
                for u in range(NU):
                    load_weights(h * NU + u)
                    if h == 0:
                        place_w1(u)
                        if u == WRING:
                            base = (GROUPS - 1) * P
                            used = NU % UPG
                            sp.dma_start(w1_rows[base + used:base + used + CTX, :],
                                         W_top1[PAIRS:PAIRS + CTX, :]).then_inc(w1_placed, 16)
                            sp.wait_ge(zeroed, 1)
                            for quad in range(4):
                                a = base + 32 * quad + used + (CTX if quad == 0 else 0)
                                n = base + 32 * (quad + 1) - a
                                sp.dma_start(w1_rows[a:a + n, :], zeros[0:n, :]).then_inc(w1_placed, 16)
                if h == 0:
                    sp.wait_ge(w1_placed, 16 * W1_DMAS)
                sp.wait_ge(prod_ready, h * NT + NT - 20 + 6)
                sp.dma_start(w1, w1_rows.rearrange("(g p) n -> p g n", p=P)).then_inc(tower_in, 16)
                sp.dma_start(w2, W_top2.rearrange("(k p) n -> p k n", p=P)).then_inc(tower_in, 16)
                sp.wait_ge(layer_out, TOWER_BLOCKS * (h + 1))
                sp.dma_start(out[h * HB:(h + 1) * HB, :].rearrange("b o -> o b"), y_sb).then_inc(y_out, 16)
            sp.wait_ge(y_out, 16 * HALVES)

        @block.gpsimd
        def _(pool):
            pool.wait_ge(ids_in, 16)

            def gather(a, n):
                h, F = divmod(a, COUPLES)
                c, x = divmod(n, 2)
                if a >= STAGES and n == 0:
                    pool.wait_ge(turned, a - STAGES + 1)
                pool.indirect_dma_start(
                    out=stage[:, a % STAGES, c, x, :], out_offset=None, in_=tables[2 * F + x][:, :],
                    in_offset=bass.IndirectOffsetOnAxis(ap=idx[:, h * BLOCKS + c, 2 * F + x:2 * F + x + 1], axis=0),
                ).then_inc(gathered[a % STAGES], 16)

            def split_lo(U):
                J = UNITS[U % NU][0]
                s = U % WRING
                pool.wait_ge(w_hi_ready, U + 1)
                pool.tensor_tensor(as_split(w_split[:, s, 1, :], J), as_loaded(w_raw[:, s, :], J),
                                   as_split(w_split[:, s, 0, :], J).bitcast(F32), ALU.subtract).then_inc(w_lo_pool, 1)

            for n in range(2 * BLOCKS):
                gather(0, n)
            pool.wait_ge(ident_made, 1)
            pool.affine_select(out=ident[:, :], in_=ident[:, :], compare_op=ALU.not_equal, fill=1.0,
                               base=0, pattern=[[-1, P]], channel_multiplier=1).then_inc(ident_made, 1)
            for a in range(1, GATHER_LEAD):
                for n in range(2 * BLOCKS):
                    gather(a, n)
            for h in range(HALVES):
                for u, (J, _) in enumerate(UNITS):
                    a = h * COUPLES + J + GATHER_LEAD
                    n, k = units_of_step[J], u - first_of_step[J]
                    if a < HALVES * COUPLES:
                        for x in range(2 * BLOCKS * k // n, 2 * BLOCKS * (k + 1) // n):
                            gather(a, x)
                    if u + W_LEAD < NU and not DVE_SPLITS[h * NU + u + W_LEAD]:
                        split_lo(h * NU + u + W_LEAD)

        @block.scalar
        def _(act):
            with nc.allow_non_contiguous_dma(reason="biases and the last layer, 1024 values"):
                act.dma_start(b1[:, :], b_top1.rearrange("(m p) -> p m", p=P)).then_inc(consts_in, 16)
                act.dma_start(b2[:, :], b_top2.rearrange("(m p) -> p m", p=P)).then_inc(consts_in, 16)
                act.dma_start(w3[:, :], W_top3.rearrange("(m p) o -> p (m o)", p=P)).then_inc(consts_in, 16)
            act.wait_ge(zeroed, 4)
            used = NU % UPG
            act.dma_start(ctx_rows[:, :, used:used + CTX],
                          dense_ctx.rearrange("(c p) x -> p c x", p=P)).then_inc(consts_in, 16)

            def split_hi(U):
                J = UNITS[U % NU][0]
                s = U % WRING
                act.wait_ge(w_in[s], w_counts[U])
                if U >= WRING:
                    act.wait_ge(T_ready, 2 * (U - WRING) + 2)
                act.copy(as_split(w_split[:, s, 0, :], J), as_loaded(w_raw[:, s, :], J)).then_inc(w_hi_ready, 1)

            def take_couple(h, F):
                act.wait_ge(turned, h * COUPLES + F + 1)
                if h and F == 0:
                    act.wait_ge(prod_ready, h * NT)
                if h and F == MLP_COUPLE:
                    act.wait_ge(y_out, 16 * h)
                act.copy(pT[:, F, :], turn[:, :]).then_inc(p_ready, 1)
                for k in q_fields(F):
                    Q, side = q_order(h, k), E * (k % 2)
                    if Q >= QRING:
                        hh, kk = divmod(Q - QRING, FIELDS - 1)
                        act.wait_ge(T_ready, hh * NT + last_tile_of_q[kk + 1] + 1)
                    act.copy(q[side:side + E, Q % QRING, :], turn[side:side + E, :]).then_inc(q_hi_ready, 1)

            def take_z(h, g):
                G = h * GROUPS + g
                act.wait_ge(summed, h * NU + min(UPG * (g + 1), NU))
                if h:
                    act.wait_ge(layer_done, TOWER_BLOCKS * h)
                act.copy(zs[:, g, 0:CHUNK], z[:, 0, :]).then_inc(z_out, 1)
                act.copy(zs[0:64, g, CHUNK:HB], z[64:P, 1, :]).then_inc(z_out, 1)
                act.copy(zs[64:P, g, CHUNK:HB], z[0:64, 1, :]).then_inc(z_out, 1)

            def tower(h):
                n = TOWER_BLOCKS * h

                def step(f):
                    nonlocal n
                    act.wait_ge(layer_done, n + 1)
                    f(turn[:, CHUNK * (n % 2):CHUNK * (n % 2 + 1)]).then_inc(layer_out, 1)
                    n += 1

                if h == 0:
                    act.wait_ge(consts_in, 64)
                for c in range(CHUNKS):
                    cols = slice(CHUNK * c, CHUNK * (c + 1))
                    for m in range(M1):
                        step(lambda t: act.activation(h1[:, m, cols], t, ACT.Relu, bias=b1[:, m:m + 1]))
                for c in range(CHUNKS):
                    cols = slice(CHUNK * c, CHUNK * (c + 1))
                    for m in range(M2):
                        step(lambda t: act.activation(h2[:, m, cols], t, ACT.Relu, bias=b2[:, m:m + 1]))
                for c in range(CHUNKS):
                    cols = slice(CHUNK * c, CHUNK * (c + 1))
                    step(lambda t: act.copy(y_sb[:, cols], t[0:1, :]))

            for h in range(HALVES):
                for U in range(h * NU, h * NU + W_LEAD):
                    split_hi(U)
                if h == 0:
                    for F in FIRST_COUPLES[h]:
                        take_couple(h, F)
                for u in range(NU):
                    if u + W_LEAD < NU:
                        split_hi(h * NU + u + W_LEAD)
                    if u - SUM_LAG + 1 > 0 and (u - SUM_LAG + 1) % UPG == 0:
                        take_z(h, (u - SUM_LAG + 1) // UPG - 1)
                    if u in turn_in[h]:
                        take_couple(h, turn_in[h][u])
                take_z(h, GROUPS - 1)
                if h + 1 < HALVES:
                    for F in FIRST_COUPLES[h + 1]:
                        take_couple(h + 1, F)
                tower(h)

        @block.vector
        def _(dve):
            def split_lo(U):
                J = UNITS[U % NU][0]
                s = U % WRING
                dve.wait_ge(w_hi_ready, U + 1)
                dve.tensor_tensor(as_split(w_split[:, s, 1, :], J), as_loaded(w_raw[:, s, :], J),
                                  as_split(w_split[:, s, 0, :], J).bitcast(F32), ALU.subtract).then_inc(w_lo_dve, 1)

            def q_lo(h, k):
                Q, side, other = q_order(h, k), E * (k % 2), E * (1 - k % 2)
                dve.wait_ge(p_ready, h * COUPLES + k // 2 + 1)
                dve.wait_ge(q_hi_ready, Q + 1)
                dve.tensor_tensor(q[other:other + E, Q % QRING, :], pT[side:side + E, k // 2, :],
                                  q[side:side + E, Q % QRING, :].bitcast(F32),
                                  ALU.subtract).then_inc(q_lo_ready, 1)

            def products(h, u):
                U = h * NU + u
                for t, (m, j) in enumerate(UNITS[u][1]):
                    tile = 2 * U + t
                    dve.wait_ge(T_ready, tile + 1)
                    dve.wait_ge(p_ready, h * COUPLES + m + 1)
                    if U >= PRING:
                        dve.wait_ge(summed, U - PRING + 1)
                    dve.tensor_tensor(prod[:, U % PRING, t, :], T[t][:, :], pT[:, m, :],
                                      ALU.mult).then_inc(prod_ready, 1)

            dve.memset(ident[:, :], 0.0).then_inc(ident_made, 1)
            dve.memset(zeros[:, :], 0.0).then_inc(zeroed, 1)
            dve.memset(ctx_rows[:, :, :], 0.0).then_inc(zeroed, 1)
            dve.memset(sel[:, :], 0.0).then_inc(zeroed, 1)
            dve.memset(sel_single[:, :], 0.0).then_inc(zeroed, 1)
            dve.wait_ge(zeroed, 4)
            dve.memset(sel[0:E, 30:31], 1.0).then_inc(consts_made, 1)
            dve.memset(sel[E:P, 31:32], 1.0).then_inc(consts_made, 1)
            dve.memset(sel_single[0:E, 30:31], 1.0).then_inc(consts_made, 1)
            for h in range(HALVES):
                for U in range(h * NU, h * NU + W_LEAD):
                    split_lo(U)
                if h == 0:
                    for F in FIRST_COUPLES[h]:
                        for k in q_fields(F):
                            q_lo(h, k)
                for u in range(NU):
                    products(h, u)
                    if u + W_LEAD < NU and DVE_SPLITS[h * NU + u + W_LEAD]:
                        split_lo(h * NU + u + W_LEAD)
                    for k in q_lo_in[h].get(u, []):
                        q_lo(h, k)
                if h + 1 < HALVES:
                    for F in FIRST_COUPLES[h + 1]:
                        for k in q_fields(F):
                            q_lo(h + 1, k)

        @block.tensor
        def _(pe):
            def turn_free(h, F):
                pe.wait_ge(p_ready, h * COUPLES + F)
                pe.wait_ge(q_hi_ready, q_order(h, 2 * F))

            def turn_couple(h, F):
                a = h * COUPLES + F
                if a:
                    turn_free(h, F)
                if h and F == len(FIRST_COUPLES[h]):
                    pe.wait_ge(layer_out, TOWER_BLOCKS * h)
                pe.wait_ge(gathered[a % STAGES], 16 * 2 * BLOCKS * (a // STAGES + 1))
                for c in range(BLOCKS):
                    mm = pe.transpose(turn[:, P * c:P * (c + 1)],
                                      stage[:, a % STAGES, c, :, :].rearrange("p x e -> p (x e)"), ident[:, :])
                mm.then_inc(turned, 1)

            def bilinear(h, u, t):
                U = h * NU + u
                tile = 2 * U + t
                Q = q_order(h, UNITS[u][1][t][1])
                wait_w_lo(pe, U)
                pe.wait_ge(q_lo_ready, Q + 1)
                if tile >= 2:
                    pe.wait_ge(prod_ready, tile - 1)
                for c in range(CHUNKS):
                    for part in (0, 1):
                        mm = pe.matmul(T[t][:, CHUNK * c:CHUNK * (c + 1)],
                                       w_split[:, U % WRING, part, P * t:P * (t + 1)],
                                       q[:, Q % QRING, CHUNK * c:CHUNK * (c + 1)],
                                       start=(part == 0), stop=(part == 1))
                mm.then_inc(T_ready, 1)

            def reduce(h, u):
                U = h * NU + u
                g, v = divmod(u, UPG)
                s, par = divmod(v, 2)
                in_group = min(UPG, NU - g * UPG)
                pe.wait_ge(prod_ready, 2 * U + 2)
                if v == 0 and (h or g):
                    pe.wait_ge(z_out, 3 * (h * GROUPS + g))
                for c in range(CHUNKS):
                    for t, (m, j) in enumerate(UNITS[u][1]):
                        quad = 2 * (par if c == 0 else 1 - par) + t
                        pick = sel_single if is_single(m, j) else sel
                        mm = pe.matmul(z[32 * quad:32 * quad + 32, c, :], pick[:, 30 - 2 * s:62 - 2 * s],
                                       prod[:, U % PRING, t, CHUNK * c:CHUNK * (c + 1)],
                                       start=(v < 2), stop=(v + 2 >= in_group))
                mm.then_inc(summed, 1)

            def add_ctx(h):
                if h == 0:
                    pe.wait_ge(consts_in, 64)
                for c in range(BLOCKS):
                    chunk, at = divmod(P * c, CHUNK)
                    quad = 0 if chunk == 0 else 2
                    pe.matmul(z[32 * quad:32 * quad + 32, chunk, at:at + P],
                              ctx_rows[:, h * BLOCKS + c, :], ident[:, :], start=False, stop=False)

            def tower(h):
                n = TOWER_BLOCKS * h
                pe.wait_ge(tower_in, 32 * (h + 1))
                if h + 1 < HALVES:
                    turn_free(h + 1, len(FIRST_COUPLES[h + 1]))
                else:
                    turn_free(h, COUPLES)

                def block_of(M, parts):
                    nonlocal n
                    if n >= TOWER_BLOCKS * h + 2:
                        pe.wait_ge(layer_out, n - 1)
                    for i, (w, x) in enumerate(parts):
                        if n == TOWER_BLOCKS * h:
                            pe.wait_ge(z_out, 3 * (GROUPS * h + i + 1))
                        mm = pe.matmul(turn[0:M, CHUNK * (n % 2):CHUNK * (n % 2 + 1)], w, x,
                                       start=(i == 0), stop=(i == len(parts) - 1))
                    mm.then_inc(layer_done, 1)
                    n += 1

                for c in range(CHUNKS):
                    cols = slice(CHUNK * c, CHUNK * (c + 1))
                    for m in range(M1):
                        block_of(P, [(w1[:, g, P * m:P * (m + 1)], zs[:, g, cols]) for g in range(GROUPS)])
                for c in range(CHUNKS):
                    cols = slice(CHUNK * c, CHUNK * (c + 1))
                    pe.wait_ge(layer_out, TOWER_BLOCKS * h + (c + 1) * M1)
                    for m in range(M2):
                        block_of(P, [(w2[:, k, P * m:P * (m + 1)], h1[:, k, cols]) for k in range(M1)])
                for c in range(CHUNKS):
                    cols = slice(CHUNK * c, CHUNK * (c + 1))
                    pe.wait_ge(layer_out, TOWER_BLOCKS * h + CHUNKS * M1 + (c + 1) * M2)
                    block_of(1, [(w3[:, k:k + 1], h2[:, k, cols]) for k in range(M2)])

            pe.wait_ge(ident_made, 2)
            pe.wait_ge(consts_made, 3)
            for h in range(HALVES):
                if h == 0:
                    for F in FIRST_COUPLES[h]:
                        turn_couple(h, F)
                for u in range(NU + SUM_LAG):
                    if u < NU:
                        bilinear(h, u, 0)
                    if u >= SUM_LAG:
                        reduce(h, u - SUM_LAG)
                    if u - SUM_LAG == (GROUPS - 1) * UPG + 1:
                        add_ctx(h)
                    if u in turn_in[h]:
                        turn_couple(h, turn_in[h][u])
                    if u < NU:
                        bilinear(h, u, 1)
                if h + 1 < HALVES:
                    for F in FIRST_COUPLES[h + 1]:
                        turn_couple(h + 1, F)
                tower(h)


def kernel(**inputs):
    import numpy as np
    from concourse import bacc
    from concourse.bass_utils import run_bass_kernel_spmd

    names = (["dense_ctx", "ids"] + [f"tbl_{f}" for f in range(FIELDS)]
             + ["W_top1", "b_top1", "W_top2", "b_top2", "W_top3", "L0_rec_param"])
    nc = bacc.Bacc("TRN2", target_bir_lowering=False, num_devices=1)
    arrays, aps = {}, {}
    for name in names:
        a = np.ascontiguousarray(inputs[name])
        arrays[f"in_{name}"] = a
        aps[name] = nc.dram_tensor(f"in_{name}", a.shape, mybir.dt.from_np(a.dtype), kind="ExternalInput").ap()
    B = inputs["dense_ctx"].shape[0]
    out = nc.dram_tensor("out_y", (B, 1), F32, kind="ExternalOutput").ap()
    tower_kernel(nc, aps["dense_ctx"], aps["ids"], [aps[f"tbl_{f}"] for f in range(FIELDS)],
                 aps["W_top1"], aps["b_top1"], aps["W_top2"], aps["b_top2"], aps["W_top3"],
                 aps["L0_rec_param"], out)
    r = run_bass_kernel_spmd(nc, [arrays], core_ids=[0])
    return r.results[0]["out_y"]
```

```python
from contextlib import ExitStack

import concourse.bass as bass
from concourse import mybir

F32 = mybir.dt.float32
F32R = mybir.dt.float32r
I32 = mybir.dt.int32
ALU = mybir.AluOpType
ACT = mybir.ActivationFunctionType

P = 128
FIELDS, E = 40, 64
HALVES = 2
COUPLES = FIELDS // 2
STEPS = COUPLES
CHUNK = 512
QRING, STAGES, WRING, PRING = 6, 7, 4, 3
GATHER_LEAD = STAGES - 1
SUM_LAG = 2
W_LEAD = 3
TOWER_GATHERS = 4
POOL_SPLITS = 6


LOOKUP_FIELDS = range(2, 11)
LOOKUP_ROWS = 1280


def pair_index(i, j):
    return i * (2 * FIELDS - 1 - i) // 2 + (j - i - 1)


def plan_units():
    units = []
    for J in range(STEPS - 1):
        units += [(J, [(m, 2 * J + 1), (m, 2 * J + 2)]) for m in range(J + 1)]
    last = STEPS - 1
    units += [(last, [(m + 1, FIELDS - 1), (m, FIELDS - 1)]) for m in range(COUPLES - 2, -1, -2)]
    return units


def tower_kernel(nc, dense_ctx, ids, tables, W_top1, b_top1, W_top2, b_top2, W_top3, param, out):
    B, CTX = dense_ctx.shape
    H1, H2 = W_top1.shape[1], W_top2.shape[1]
    PAIRS = param.shape[1]
    HB = B // HALVES
    BLOCKS = HB // P
    CHUNKS = HB // CHUNK
    M1, M2 = H1 // P, H2 // P

    UNITS = plan_units()
    NU = len(UNITS)
    NT = 2 * NU
    UPG = 32
    GROUPS = -(-NU // UPG)
    first_of_step = {}
    units_of_step = {}
    for u, (J, _) in enumerate(UNITS):
        first_of_step.setdefault(J, u)
        units_of_step[J] = units_of_step.get(J, 0) + 1
    last_tile_of_q = {}
    for u, (_, tiles) in enumerate(UNITS):
        for t, (m, j) in enumerate(tiles):
            last_tile_of_q[j] = 2 * u + t

    def is_single(m, j):
        return 2 * m + 1 == j

    FIRST_COUPLES = [range(2), range(5)]
    turn_in = [{}, {}]
    for J in range(STEPS - 2):
        n = units_of_step[J]
        turn_in[0][first_of_step[J] + n - (1 if J < 3 else 2 if J < 5 else 3 if J < 8 else 5)] = J + 2
    for J in range(2, STEPS - 3):
        turn_in[1][first_of_step[J]] = J + 3

    q_hi_in, q_lo_in = [{}, {}], [{}, {}]
    for h in range(HALVES):
        turn_slot = {F: u for u, F in turn_in[h].items()}
        at = lo = -1
        for k in range(1, FIELDS):
            step = (k - 1) // 2
            first = first_of_step[step]
            if k // 2 not in FIRST_COUPLES[h] or k > QRING:
                at = max(at, turn_slot.get(k // 2, 0), first - (7 if k % 2 else 4),
                         first_of_step[step - 2] if step > 2 else 0)
                assert at < first
            q_hi_in[h].setdefault(at, []).append(k)
            for piece in range(CHUNKS):
                lo = max(lo, min(at + 1 + piece, first - 1) if at >= 0 else -1)
                q_lo_in[h].setdefault(lo, []).append((k, piece))

    LOOKUPS = [f for f in LOOKUP_FIELDS if tables[f].shape[0] <= LOOKUP_ROWS]
    SLICES = {f: -(-tables[f].shape[0] // P) for f in LOOKUPS}
    SLICE_ROWS = tables[LOOKUPS[0]].shape[0] // SLICES[LOOKUPS[0]]
    assert all(SLICES[f] * SLICE_ROWS == tables[f].shape[0] for f in LOOKUPS) and len(LOOKUPS) == 4
    slices_before = {f: sum(SLICES[x] for x in LOOKUPS[:n]) for n, f in enumerate(LOOKUPS)}
    ONEHOTS = 4
    PARTS = 10 * 2 * E
    assert all(SLICES[f] * 2 * E <= PARTS for f in LOOKUPS)

    def gathered_fields(h, F):
        return [x for x in (0, 1) if h or 2 * F + x not in LOOKUPS]

    def q_order(h, k):
        return h * (FIELDS - 1) + max(k - 1, 0)

    DVE_SPLITS = [u < first_of_step[POOL_SPLITS] for u in range(NU)] + [u < W_LEAD for u in range(NU)]

    ctx = ExitStack()
    with ctx:
        def sb(name, shape, dt=F32):
            return ctx.enter_context(nc.sbuf_tensor(name, shape, dt))

        def psum(name, shape):
            return ctx.enter_context(nc.psum_tensor(name, shape, F32))

        def sem(name):
            return ctx.enter_context(nc.semaphore(name))

        idx = sb("idx", [P, B // P, FIELDS], I32)
        stage = sb("stage", [P, STAGES, BLOCKS, 2, E])
        pT = sb("pT", [P, COUPLES, HB])
        q = sb("q", [P, QRING, HB], F32R)
        w_raw = sb("w_raw", [P, WRING, 4 * E])
        w_split = sb("w_split", [P, WRING, 2, 4 * E], F32R)
        prod = sb("prod", [P, PRING, 2, HB])
        with nc.sbuf_tensor("lookup_parts", [P, 2 * PARTS + ONEHOTS * HB], F32R) as lookup_parts:
            pass
        zs = sb("zs", [P, GROUPS, HB])
        sel = sb("sel", [P, 62])
        sel_single = sb("sel_single", [P, 62])
        ident = sb("ident", [P, P])
        ctx_rows = sb("ctx_rows", [P, B // P, 32])
        zeros = sb("zeros", [32, H1])
        b1 = sb("b1", [P, M1])
        b2 = sb("b2", [P, M2])
        w3 = sb("w3", [P, M2])
        MLP_COUPLE = 8
        y_sb = pT[0:1, 8, :]
        h2 = pT[:, 9:11, :]
        h1 = pT[:, 11:15, :]
        w2 = pT[:, 15, 0:M1 * H2].rearrange("p (k n) -> p k n", n=H2)
        w1 = pT[:, 16:20, :].rearrange("p a b -> p (a b)")[:, 0:GROUPS * H1].rearrange(
            "p (g n) -> p g n", n=H1)
        def looked_table(n):
            return pT[0:SLICE_ROWS, 8 + n, :]

        def looked_ids(n):
            return pT[:, 12 + n, :]

        def looked_parts(n):
            return lookup_parts[0:SLICE_ROWS, PARTS * (n % 2):PARTS * (n % 2 + 1)]

        def looked_part(n, f, part):
            return looked_parts(n)[:, 0:2 * E * SLICES[f]].rearrange("p (t x e) -> p t x e", x=2, e=E)[:, :, part, :]

        def as_slices(ap, f):
            return ap[:, 0:E * SLICES[f]].rearrange("p (t e) -> p t e", e=E)

        def onehot(i):
            at = PARTS * 2 + HB * (i % ONEHOTS)
            return lookup_parts[0:SLICE_ROWS, at:at + HB]

        def diag(n):
            return pT[:, 18 + n % 2, :]

        ids_f = sb("ids_f", [P, len(LOOKUPS), BLOCKS])
        ones = sb("ones", [P, P])
        row_int = sb("row_int", [P, 16], I32)
        row_of = sb("row_of", [P, 16])
        w1_rows = nc.dram_tensor("w1_rows", [GROUPS * P, H1], F32, kind="Internal").ap()

        T = [psum(f"T{i}", [P, HB]) for i in range(2)]
        turn = psum("turn", [P, HB])
        z = psum("z", [P, CHUNKS, CHUNK])

        ids_in = sem("ids_in")
        consts_in = sem("consts_in")
        consts_made = sem("consts_made")
        zeroed = sem("zeroed")
        ident_made = sem("ident_made")
        gathered = [sem(f"gathered{i}") for i in range(STAGES)]
        turned = sem("turned")
        p_ready = sem("p_ready")
        q_hi_ready = sem("q_hi_ready")
        q_lo_ready = sem("q_lo_ready")
        w_in = [sem(f"w_in{i}") for i in range(WRING)]
        w_hi_ready = sem("w_hi_ready")
        w_lo_dve = sem("w_lo_dve")
        w_lo_pool = sem("w_lo_pool")
        T_ready = sem("T_ready")
        prod_ready = sem("prod_ready")
        summed = sem("summed")
        z_out = sem("z_out")
        w1_placed = sem("w1_placed")
        tower_in = sem("tower_in")
        layer_done = sem("layer_done")
        layer_out = sem("layer_out")
        y_out = sem("y_out")
        table_in = [sem(f"table_in{n}") for n in range(len(LOOKUPS))]
        ids_cast = sem("ids_cast")
        rows_numbered = sem("rows_numbered")
        diag_made = sem("diag_made")
        ids_spread = sem("ids_spread")
        ids_row = sem("ids_row")
        table_hi = sem("table_hi")
        table_lo = sem("table_lo")
        onehot_made = sem("onehot_made")
        onehot_used = sem("onehot_used")
        looked_out = sem("looked_out")
        looked_up = sem("looked_up")

        block = ctx.enter_context(nc.Block())

        TOWER_BLOCKS = CHUNKS * (M1 + M2 + 1)
        W1_DMAS = (STEPS - 1) * STEPS // 2 + COUPLES + 1 + 4

        def wait_w_lo(eng, U):
            n = sum(DVE_SPLITS[:U + 1])
            if DVE_SPLITS[U]:
                eng.wait_ge(w_lo_dve, n)
            else:
                eng.wait_ge(w_lo_pool, U + 1 - n)

        w_counts = {}
        total = [0] * WRING
        for U in range(HALVES * NU):
            total[U % WRING] += 32 if UNITS[U % NU][0] < STEPS - 1 else 64
            w_counts[U] = total[U % WRING]

        gathers_of, total = {}, [0] * STAGES
        for a in range(HALVES * COUPLES):
            total[a % STAGES] += BLOCKS * len(gathered_fields(*divmod(a, COUPLES)))
            gathers_of[a] = 16 * total[a % STAGES]

        def ids_bank(n):
            return T[1][:, :] if n == 1 else T[0][:, :]

        def looked_sums(n):
            return z[:, :, :].rearrange("p c n -> p (c n)") if n % 2 == 0 else T[1][:, :]

        def tower_bank(n):
            return T[n // 2 % 2][:, CHUNK * (n % 2):CHUNK * (n % 2 + 1)]

        def as_loaded(ap, J):
            return ap if J == STEPS - 1 else ap.rearrange("p (i j e) -> p i j e", j=2, i=2)

        def as_split(ap, J):
            return ap if J == STEPS - 1 else ap.rearrange("p (j i e) -> p i j e", j=2, i=2)

        @block.sync
        def _(sp):
            sp.dma_start(idx[:, :, :], ids.rearrange("(c p) f -> p c f", p=P)).then_inc(ids_in, 16)

            for n, f in enumerate(LOOKUPS):
                sp.dma_start(as_slices(looked_table(n), f),
                             tables[f].rearrange("(t p) e -> p t e", p=SLICE_ROWS)).then_inc(table_in[n], 16)

            def load_weights(U):
                J, tiles = UNITS[U % NU]
                s = U % WRING
                if U >= WRING:
                    wait_w_lo(sp, U - WRING)
                for half in (0, E):
                    dst = w_raw[half:half + E, s, :]
                    if J < STEPS - 1:
                        m = tiles[0][0]
                        at, step = pair_index(2 * m, 2 * J + 1), FIELDS - 2 - 2 * m
                        src = bass.AP(param.tensor, at * E,
                                      [[PAIRS * E, E], [step * E, 2], [1, 2 * E]])
                        sp.dma_start(dst.rearrange("p (i x) -> p i x", i=2), src).then_inc(w_in[s], 16)
                    else:
                        for t, (m, j) in enumerate(tiles):
                            at, step = pair_index(2 * m, j), FIELDS - 2 - 2 * m
                            src = bass.AP(param.tensor, at * E,
                                          [[PAIRS * E, E], [step * E, 2], [1, E]])
                            sp.dma_start(dst[:, 2 * E * t:2 * E * (t + 1)].rearrange(
                                "p (i e) -> p i e", i=2), src).then_inc(w_in[s], 16)

            def place_w1(u):
                J, tiles = UNITS[u]
                g, v = divmod(u, UPG)
                s, par = divmod(v, 2)
                row = g * P + 64 * par + 2 * s
                if J < STEPS - 1:
                    m = tiles[0][0]
                    step = FIELDS - 2 - 2 * m
                    src = bass.AP(W_top1.tensor, pair_index(2 * m, 2 * J + 1) * H1,
                                  [[H1, 2], [step * H1, 2], [1, H1]])
                    dst = bass.AP(w1_rows.tensor, row * H1, [[32 * H1, 2], [H1, 2], [1, H1]])
                    sp.dma_start(dst, src).then_inc(w1_placed, 16)
                else:
                    for t, (m, j) in enumerate(tiles):
                        step = FIELDS - 2 - 2 * m
                        src = bass.AP(W_top1.tensor, pair_index(2 * m, j) * H1, [[step * H1, 2], [1, H1]])
                        sp.dma_start(w1_rows[row + 32 * t:row + 32 * t + 2, :], src).then_inc(w1_placed, 16)

            def load_tower(h):
                if h == 0:
                    sp.wait_ge(w1_placed, 16 * W1_DMAS)
                sp.wait_ge(prod_ready, h * NT + NT - 20 + 6)
                sp.dma_start(w1, w1_rows.rearrange("(g p) n -> p g n", p=P)).then_inc(tower_in, 16)
                sp.dma_start(w2, W_top2.rearrange("(k p) n -> p k n", p=P)).then_inc(tower_in, 16)

            for U in range(HALVES * NU):
                load_weights(U)
                if U < NU:
                    place_w1(U)
                if U == WRING:
                    base = (GROUPS - 1) * P
                    used = NU % UPG
                    sp.dma_start(w1_rows[base + used:base + used + CTX, :],
                                 W_top1[PAIRS:PAIRS + CTX, :]).then_inc(w1_placed, 16)
                    sp.wait_ge(zeroed, 1)
                    for quad in range(4):
                        a = base + 32 * quad + used + (CTX if quad == 0 else 0)
                        n = base + 32 * (quad + 1) - a
                        sp.dma_start(w1_rows[a:a + n, :], zeros[0:n, :]).then_inc(w1_placed, 16)
                if U == NU + W_LEAD - 1:
                    load_tower(0)
            load_tower(1)

        @block.gpsimd
        def _(pool):
            pool.iota(row_int[:, :], pattern=[[SLICE_ROWS, 16]], base=0, channel_multiplier=1
                      ).then_inc(rows_numbered, 1)
            pool.wait_ge(ident_made, 1)
            pool.affine_select(out=ident[:, :], in_=ident[:, :], compare_op=ALU.not_equal, fill=1.0,
                               base=0, pattern=[[-1, P]], channel_multiplier=1).then_inc(ident_made, 1)
            pool.wait_ge(ids_in, 16)

            def gather(a, n):
                h, F = divmod(a, COUPLES)
                c, x = divmod(n, 2)
                if x not in gathered_fields(h, F):
                    return
                if a >= STAGES and n == 0:
                    pool.wait_ge(turned, a - STAGES + 1)
                pool.indirect_dma_start(
                    out=stage[:, a % STAGES, c, x, :], out_offset=None, in_=tables[2 * F + x][:, :],
                    in_offset=bass.IndirectOffsetOnAxis(ap=idx[:, h * BLOCKS + c, 2 * F + x:2 * F + x + 1], axis=0),
                ).then_inc(gathered[a % STAGES], 16)

            def split_lo(U):
                J = UNITS[U % NU][0]
                s = U % WRING
                pool.wait_ge(w_hi_ready, U + 1)
                pool.tensor_tensor(as_split(w_split[:, s, 1, :], J), as_loaded(w_raw[:, s, :], J),
                                   as_split(w_split[:, s, 0, :], J).bitcast(F32), ALU.subtract).then_inc(w_lo_pool, 1)

            for a in range(GATHER_LEAD):
                for n in range(2 * BLOCKS):
                    gather(a, n)
            n_of_couple, done = 2 * BLOCKS, 0
            BEHIND = (POOL_SPLITS + 3 - GATHER_LEAD) * n_of_couple
            todo = [(a, n) for a in range(GATHER_LEAD, HALVES * COUPLES) for n in range(2 * BLOCKS)]
            for U in range(HALVES * NU):
                h, u = divmod(U, NU)
                J = UNITS[u][0]
                n, k = units_of_step[J], u - first_of_step[J]
                if U + W_LEAD < HALVES * NU and not DVE_SPLITS[U + W_LEAD]:
                    split_lo(U + W_LEAD)
                if h == 0:
                    upto = min(J * n_of_couple + n_of_couple * (k + 1) // n,
                               BEHIND + max(0, 15 * (u - first_of_step[POOL_SPLITS]) // 8))
                else:
                    upto = (STEPS + TOWER_GATHERS) * n_of_couple + 3 * (u + 1) // 2
                while done < min(upto, len(todo)):
                    gather(*todo[done])
                    done += 1
                if U == NU - 1:
                    while done < (STEPS + TOWER_GATHERS) * n_of_couple:
                        gather(*todo[done])
                        done += 1

        @block.scalar
        def _(act):
            with nc.allow_non_contiguous_dma(reason="biases and the last layer, 1024 values"):
                act.dma_start(b1[:, :], b_top1.rearrange("(m p) -> p m", p=P)).then_inc(consts_in, 16)
                act.dma_start(b2[:, :], b_top2.rearrange("(m p) -> p m", p=P)).then_inc(consts_in, 16)
                act.dma_start(w3[:, :], W_top3.rearrange("(m p) o -> p (m o)", p=P)).then_inc(consts_in, 16)
            act.wait_ge(zeroed, 4)
            used = NU % UPG
            act.dma_start(ctx_rows[:, :, used:used + CTX],
                          dense_ctx.rearrange("(c p) x -> p c x", p=P)).then_inc(consts_in, 16)

            def split_hi(U):
                J = UNITS[U % NU][0]
                s = U % WRING
                act.wait_ge(w_in[s], w_counts[U])
                if U >= WRING:
                    act.wait_ge(T_ready, 2 * (U - WRING) + 2)
                act.copy(as_split(w_split[:, s, 0, :], J), as_loaded(w_raw[:, s, :], J)).then_inc(w_hi_ready, 1)

            def take_couple(h, F):
                act.wait_ge(turned, h * COUPLES + F + 1)
                if h and F == 0:
                    act.wait_ge(prod_ready, h * NT)
                if h and F == MLP_COUPLE:
                    act.wait_ge(y_out, 16 * h)
                x = gathered_fields(h, F)
                part = slice(E * x[0], E * (x[-1] + 1))
                act.copy(pT[part, F, :], turn[0:E * len(x), :]).then_inc(p_ready, 1)

            def take_q_hi(h, k):
                Q, side = q_order(h, k), E * (k % 2)
                act.wait_ge(p_ready, h * COUPLES + k // 2 + 1)
                if h == 0 and k in LOOKUPS:
                    act.wait_ge(looked_up, LOOKUPS.index(k) + 1)
                if Q >= QRING:
                    hh, kk = divmod(Q - QRING, FIELDS - 1)
                    act.wait_ge(T_ready, hh * NT + last_tile_of_q[kk + 1] + 1)
                act.copy(q[side:side + E, Q % QRING, :], pT[side:side + E, k // 2, :]).then_inc(q_hi_ready, 1)

            def take_first(h, F):
                take_couple(h, F)
                for k in q_hi_in[h][-1]:
                    if k // 2 == F:
                        take_q_hi(h, k)

            def take_z(h, g):
                G = h * GROUPS + g
                act.wait_ge(summed, h * NU + min(UPG * (g + 1), NU))
                if h:
                    act.wait_ge(layer_done, TOWER_BLOCKS * h)
                act.copy(zs[:, g, 0:CHUNK], z[:, 0, :]).then_inc(z_out, 1)
                act.copy(zs[0:64, g, CHUNK:HB], z[64:P, 1, :]).then_inc(z_out, 1)
                act.copy(zs[64:P, g, CHUNK:HB], z[0:64, 1, :]).then_inc(z_out, 1)

            def tower(h):
                n = TOWER_BLOCKS * h

                def step(f):
                    nonlocal n
                    act.wait_ge(layer_done, n + 1)
                    f(tower_bank(n)).then_inc(layer_out, 1)
                    n += 1

                if h == 0:
                    act.wait_ge(consts_in, 64)
                for c in range(CHUNKS):
                    cols = slice(CHUNK * c, CHUNK * (c + 1))
                    for m in range(M1):
                        step(lambda t: act.activation(h1[:, m, cols], t, ACT.Relu, bias=b1[:, m:m + 1]))
                        F = c * M1 + m + 1
                        if h + 1 < HALVES and F in FIRST_COUPLES[h + 1]:
                            take_first(h + 1, F)
                for c in range(CHUNKS):
                    cols = slice(CHUNK * c, CHUNK * (c + 1))
                    for m in range(M2):
                        step(lambda t: act.activation(h2[:, m, cols], t, ACT.Relu, bias=b2[:, m:m + 1]))
                for c in range(CHUNKS):
                    cols = slice(CHUNK * c, CHUNK * (c + 1))
                    step(lambda t: act.copy(y_sb[:, cols], t[32 * c:32 * c + 1, :]))
                act.wait_ge(layer_out, TOWER_BLOCKS * (h + 1))
                act.dma_start(out[h * HB:(h + 1) * HB, :].rearrange("b o -> o b"), y_sb).then_inc(y_out, 16)

            def make_diag(n):
                act.wait_ge(ids_cast, len(LOOKUPS))
                act.wait_ge(ident_made, 2)
                if n >= 2:
                    act.wait_ge(ids_spread, n - 1)
                for c in range(BLOCKS):
                    act.activation(diag(n)[:, P * c:P * (c + 1)], ident[:, :], ACT.Copy,
                                   scale=ids_f[:, n, c:c + 1]).then_inc(diag_made, 1)

            def take_ids(n):
                act.wait_ge(ids_spread, n + 1)
                act.copy(looked_ids(n), ids_bank(n)).then_inc(ids_row, 1)

            def split_table(n, f):
                act.wait_ge(table_in[n], 16)
                if n >= 2:
                    act.wait_ge(onehot_used, slices_before[LOOKUPS[n - 1]])
                act.copy(looked_part(n, f, 0), as_slices(looked_table(n), f)).then_inc(table_hi, 1)

            def take_looked(n, f):
                act.wait_ge(onehot_used, slices_before[f] + SLICES[f])
                act.copy(looked_ids(n)[E:P, :], looked_sums(n)[0:E, :]).then_inc(looked_out, 1)

            for n in range(2):
                make_diag(n)
            for n in range(2):
                take_ids(n)
                split_table(n, LOOKUPS[n])
            for n in range(2, len(LOOKUPS)):
                make_diag(n)
                take_ids(n)
            for n, f in enumerate(LOOKUPS):
                take_looked(n, f)
                if n + 2 < len(LOOKUPS):
                    split_table(n + 2, LOOKUPS[n + 2])
                if n == 1:
                    take_first(0, 0)
                if n == 2:
                    for U in range(W_LEAD):
                        split_hi(U)
            take_first(0, 1)
            for h in range(HALVES):
                for u in range(NU):
                    if h * NU + u + W_LEAD < HALVES * NU:
                        split_hi(h * NU + u + W_LEAD)
                    if u - SUM_LAG + 1 > 0 and (u - SUM_LAG + 1) % UPG == 0:
                        take_z(h, (u - SUM_LAG + 1) // UPG - 1)
                    if u in turn_in[h]:
                        take_couple(h, turn_in[h][u])
                    for k in q_hi_in[h].get(u, []):
                        take_q_hi(h, k)
                if h + 1 < HALVES:
                    take_first(h + 1, 0)
                take_z(h, GROUPS - 1)
                tower(h)
            act.wait_ge(y_out, 16 * HALVES)

        @block.vector
        def _(dve):
            def split_lo(U):
                J = UNITS[U % NU][0]
                s = U % WRING
                dve.wait_ge(w_hi_ready, U + 1)
                dve.tensor_tensor(as_split(w_split[:, s, 1, :], J), as_loaded(w_raw[:, s, :], J),
                                  as_split(w_split[:, s, 0, :], J).bitcast(F32), ALU.subtract).then_inc(w_lo_dve, 1)

            def q_lo(h, k, piece):
                Q, side, other = q_order(h, k), E * (k % 2), E * (1 - k % 2)
                cols = slice(CHUNK * piece, CHUNK * (piece + 1))
                dve.wait_ge(q_hi_ready, Q + 1)
                dve.tensor_tensor(q[other:other + E, Q % QRING, cols], pT[side:side + E, k // 2, cols],
                                  q[side:side + E, Q % QRING, cols].bitcast(F32),
                                  ALU.subtract).then_inc(q_lo_ready, 1)

            def products(h, u, t):
                U = h * NU + u
                m, j = UNITS[u][1][t]
                tile = 2 * U + t
                dve.wait_ge(T_ready, tile + 1)
                dve.wait_ge(p_ready, h * COUPLES + m + 1)
                if U >= PRING:
                    dve.wait_ge(summed, U - PRING + 1)
                dve.tensor_tensor(prod[:, U % PRING, t, :], T[t][:, :], pT[:, m, :],
                                  ALU.mult).then_inc(prod_ready, 1)

            def split_table(n, f):
                dve.wait_ge(table_hi, n + 1)
                dve.tensor_tensor(looked_part(n, f, 1), as_slices(looked_table(n), f),
                                  looked_part(n, f, 0).bitcast(F32), ALU.subtract).then_inc(table_lo, 1)

            def add_parts(n, f):
                dve.wait_ge(looked_out, n + 1)
                dve.tensor_tensor(pT[E * (f % 2):E * (f % 2 + 1), f // 2, :], looked_sums(n)[E:P, :],
                                  looked_ids(n)[E:P, :], ALU.add).then_inc(looked_up, 1)

            def make_onehots(n, f):
                dve.wait_ge(ids_row, n + 1)
                for t in range(SLICES[f]):
                    if t == ONEHOTS and n:
                        add_parts(n - 1, LOOKUPS[n - 1])
                    i = slices_before[f] + t
                    if i >= ONEHOTS:
                        dve.wait_ge(onehot_used, i - ONEHOTS + 1)
                    dve.tensor_scalar(onehot(i), looked_ids(n)[0:SLICE_ROWS, :], row_of[0:SLICE_ROWS, t:t + 1],
                                      None, ALU.is_equal).then_inc(onehot_made, 1)

            dve.memset(ident[:, :], 0.0).then_inc(ident_made, 1)
            dve.memset(ones[:, :], 1.0).then_inc(consts_made, 1)
            dve.memset(zeros[:, :], 0.0).then_inc(zeroed, 1)
            dve.memset(ctx_rows[:, :, :], 0.0).then_inc(zeroed, 1)
            dve.memset(sel[:, :], 0.0).then_inc(zeroed, 1)
            dve.memset(sel_single[:, :], 0.0).then_inc(zeroed, 1)
            dve.wait_ge(zeroed, 4)
            dve.memset(sel[0:E, 30:31], 1.0).then_inc(consts_made, 1)
            dve.memset(sel[E:P, 31:32], 1.0).then_inc(consts_made, 1)
            dve.memset(sel_single[0:E, 30:31], 1.0).then_inc(consts_made, 1)
            dve.wait_ge(rows_numbered, 1)
            dve.tensor_copy(row_of[:, :], row_int[:, :]).then_inc(rows_numbered, 1)
            dve.wait_ge(ids_in, 16)
            for n, f in enumerate(LOOKUPS):
                dve.tensor_copy(ids_f[:, n, :], idx[:, 0:BLOCKS, f]).then_inc(ids_cast, 1)
            dve.wait_ge(rows_numbered, 2)
            for n, f in enumerate(LOOKUPS):
                split_table(n, f)
                make_onehots(n, f)
            add_parts(n, f)
            for U in range(W_LEAD):
                split_lo(U)
            for h in range(HALVES):
                for k, piece in q_lo_in[h][-1]:
                    q_lo(h, k, piece)
                for u in range(NU):
                    products(h, u, 0)
                    U = h * NU + u + W_LEAD
                    if U < HALVES * NU and DVE_SPLITS[U]:
                        split_lo(U)
                    pieces = q_lo_in[h].get(u, [])
                    for k, piece in pieces:
                        if k not in q_hi_in[h].get(u, []):
                            q_lo(h, k, piece)
                    products(h, u, 1)
                    for k, piece in pieces:
                        if k in q_hi_in[h].get(u, []):
                            q_lo(h, k, piece)

        @block.tensor
        def _(pe):
            def turn_couple(h, F):
                a = h * COUPLES + F
                if a:
                    pe.wait_ge(p_ready, a)
                pe.wait_ge(gathered[a % STAGES], gathers_of[a])
                x = gathered_fields(h, F)
                x = slice(x[0], x[-1] + 1)
                for c in range(BLOCKS):
                    mm = pe.transpose(turn[0:E * (x.stop - x.start), P * c:P * (c + 1)],
                                      stage[:, a % STAGES, c, x, :].rearrange("p x e -> p (x e)"), ident[:, :])
                mm.then_inc(turned, 1)

            def bilinear(h, u, t):
                U = h * NU + u
                tile = 2 * U + t
                Q = q_order(h, UNITS[u][1][t][1])
                wait_w_lo(pe, U)
                pe.wait_ge(q_lo_ready, CHUNKS * (Q + 1))
                if h and u == 0:
                    pe.wait_ge(layer_out, TOWER_BLOCKS * h)
                if tile >= 2:
                    pe.wait_ge(prod_ready, tile - 1)
                for c in range(CHUNKS):
                    for part in (0, 1):
                        mm = pe.matmul(T[t][:, CHUNK * c:CHUNK * (c + 1)],
                                       w_split[:, U % WRING, part, P * t:P * (t + 1)],
                                       q[:, Q % QRING, CHUNK * c:CHUNK * (c + 1)],
                                       start=(part == 0), stop=(part == 1))
                mm.then_inc(T_ready, 1)

            def reduce(h, u):
                U = h * NU + u
                g, v = divmod(u, UPG)
                s, par = divmod(v, 2)
                in_group = min(UPG, NU - g * UPG)
                pe.wait_ge(prod_ready, 2 * U + 2)
                if v == 0 and (h or g):
                    pe.wait_ge(z_out, 3 * (h * GROUPS + g))
                for c in range(CHUNKS):
                    for t, (m, j) in enumerate(UNITS[u][1]):
                        quad = 2 * (par if c == 0 else 1 - par) + t
                        pick = sel_single if is_single(m, j) else sel
                        mm = pe.matmul(z[32 * quad:32 * quad + 32, c, :], pick[:, 30 - 2 * s:62 - 2 * s],
                                       prod[:, U % PRING, t, CHUNK * c:CHUNK * (c + 1)],
                                       start=(v < 2), stop=(v + 2 >= in_group))
                mm.then_inc(summed, 1)

            def add_ctx(h):
                if h == 0:
                    pe.wait_ge(consts_in, 64)
                for c in range(BLOCKS):
                    chunk, at = divmod(P * c, CHUNK)
                    quad = 0 if chunk == 0 else 2
                    pe.matmul(z[32 * quad:32 * quad + 32, chunk, at:at + P],
                              ctx_rows[:, h * BLOCKS + c, :], ident[:, :], start=False, stop=False)

            def tower(h):
                n = TOWER_BLOCKS * h
                pe.wait_ge(tower_in, 32 * (h + 1))
                pe.wait_ge(prod_ready, NT * (h + 1))

                def block_of(M, parts):
                    nonlocal n
                    if n >= TOWER_BLOCKS * h + 4:
                        pe.wait_ge(layer_out, n - 3)
                    for i, (w, x) in enumerate(parts):
                        if n == TOWER_BLOCKS * h:
                            pe.wait_ge(z_out, 3 * (GROUPS * h + i + 1))
                        mm = pe.matmul(tower_bank(n)[0:M, :], w, x,
                                       start=(i == 0), stop=(i == len(parts) - 1))
                    mm.then_inc(layer_done, 1)
                    n += 1

                for c in range(CHUNKS):
                    cols = slice(CHUNK * c, CHUNK * (c + 1))
                    for m in range(M1):
                        F = c * M1 + m
                        if F and h + 1 < HALVES and F in FIRST_COUPLES[h + 1]:
                            turn_couple(h + 1, F)
                        block_of(P, [(w1[:, g, P * m:P * (m + 1)], zs[:, g, cols]) for g in range(GROUPS)])
                for c in range(CHUNKS):
                    cols = slice(CHUNK * c, CHUNK * (c + 1))
                    pe.wait_ge(layer_out, TOWER_BLOCKS * h + (c + 1) * M1)
                    for m in range(M2):
                        block_of(P, [(w2[:, k, P * m:P * (m + 1)], h1[:, k, cols]) for k in range(M1)])
                pe.wait_ge(layer_out, TOWER_BLOCKS * h + CHUNKS * (M1 + M2))
                for k in range(M2):
                    for c in range(CHUNKS):
                        mm = pe.matmul(tower_bank(n + c)[32 * c:32 * c + 1, :], w3[:, k:k + 1],
                                       h2[:, k, CHUNK * c:CHUNK * (c + 1)], start=(k == 0), stop=(k + 1 == M2))
                mm.then_inc(layer_done, CHUNKS)

            pe.wait_ge(ident_made, 2)
            pe.wait_ge(consts_made, 4)

            def spread_ids(n):
                if n >= 2:
                    pe.wait_ge(ids_row, n)
                for c in range(CHUNKS):
                    cols = slice(CHUNK * c, CHUNK * (c + 1))
                    pe.wait_ge(diag_made, BLOCKS * n + BLOCKS // CHUNKS * (c + 1))
                    mm = pe.matmul(ids_bank(n)[:, cols], ones[:, :], diag(n)[:, cols], start=True, stop=True)
                mm.then_inc(ids_spread, 1)

            def look_up(n, f):
                if n == 1:
                    pe.wait_ge(ids_row, 2)
                if n >= 2:
                    pe.wait_ge(looked_up, n - 1)
                pe.wait_ge(table_lo, n + 1)
                for t in range(SLICES[f]):
                    i = slices_before[f] + t
                    pe.wait_ge(onehot_made, i + 1)
                    for c in range(CHUNKS):
                        mm = pe.matmul(looked_sums(n)[:, CHUNK * c:CHUNK * (c + 1)],
                                       looked_parts(n)[:, 2 * E * t:2 * E * (t + 1)],
                                       onehot(i)[:, CHUNK * c:CHUNK * (c + 1)],
                                       start=(t == 0), stop=(t + 1 == SLICES[f]))
                    mm.then_inc(onehot_used, 1)

            for n in range(3):
                spread_ids(n)
            for n, f in enumerate(LOOKUPS):
                look_up(n, f)
                if n == 0:
                    spread_ids(3)
                if n == 1:
                    turn_couple(0, 0)
            turn_couple(0, 1)
            pe.wait_ge(ids_row, len(LOOKUPS))
            pe.wait_ge(looked_up, len(LOOKUPS))
            for h in range(HALVES):
                for u in range(NU + SUM_LAG):
                    if u < NU:
                        bilinear(h, u, 0)
                    if u == NU + SUM_LAG - 1 and h + 1 < HALVES:
                        turn_couple(h + 1, 0)
                    if u >= SUM_LAG:
                        reduce(h, u - SUM_LAG)
                    if u - SUM_LAG == (GROUPS - 1) * UPG + 1:
                        add_ctx(h)
                    if u in turn_in[h]:
                        turn_couple(h, turn_in[h][u])
                    if u < NU:
                        bilinear(h, u, 1)
                tower(h)


def kernel(**inputs):
    import numpy as np
    from concourse import bacc
    from concourse.bass_utils import run_bass_kernel_spmd

    names = (["dense_ctx", "ids"] + [f"tbl_{f}" for f in range(FIELDS)]
             + ["W_top1", "b_top1", "W_top2", "b_top2", "W_top3", "L0_rec_param"])
    nc = bacc.Bacc("TRN2", target_bir_lowering=False, num_devices=1)
    arrays, aps = {}, {}
    for name in names:
        a = np.ascontiguousarray(inputs[name])
        arrays[f"in_{name}"] = a
        aps[name] = nc.dram_tensor(f"in_{name}", a.shape, mybir.dt.from_np(a.dtype), kind="ExternalInput").ap()
    B = inputs["dense_ctx"].shape[0]
    out = nc.dram_tensor("out_y", (B, 1), F32, kind="ExternalOutput").ap()
    tower_kernel(nc, aps["dense_ctx"], aps["ids"], [aps[f"tbl_{f}"] for f in range(FIELDS)],
                 aps["W_top1"], aps["b_top1"], aps["W_top2"], aps["b_top2"], aps["W_top3"],
                 aps["L0_rec_param"], out)
    r = run_bass_kernel_spmd(nc, [arrays], core_ids=[0])
    return r.results[0]["out_y"]
```
